# Optimizing a Trainium2 kernel written in Bass

```python
import numpy as np
import jax
import jax.numpy as jnp

def _softmax(x, axis=-1):
    return jax.nn.softmax(x, axis=axis)

def _gelu(x):
    return jax.nn.gelu(x, approximate=True)

def _silu(x):
    return jax.nn.silu(x)

def _sigmoid(x):
    return jax.nn.sigmoid(x)

def _layernorm(x, axis=-1, eps=1e-05):
    m = jnp.mean(x, axis=axis, keepdims=True)
    v = jnp.var(x, axis=axis, keepdims=True)
    return (x - m) / jnp.sqrt(v + eps)

def _scatter_add(tgt, idx, src, axis=0):
    return tgt.at[idx].add(src)

def _segment_sum(src, seg, n):
    return jax.ops.segment_sum(src, seg, n)
kernel_name = 'mk_adj_resnorm_d2_adj_r2_e01957'

def setup_inputs(seed: int=0):
    np.random.seed(seed)
    _w = jnp.asarray

    def _rec_inputs():
        import jax
        import jax.numpy as jnp
        _gk = jax.random.key(seed)
        x = -0.0002928 + 1 * jax.random.normal(jax.random.fold_in(_gk, 1), (2048, 512), jnp.float32)
        _a = jax.random.bernoulli(jax.random.fold_in(_gk, 2), 0.000976562, (2048, 2048))
        _a = jnp.logical_or(_a, jnp.swapaxes(_a, -1, -2))
        _a = jnp.logical_or(_a, jnp.eye(2048, dtype=bool))
        _af = _a.astype(jnp.float32)
        adj = _af
        return (x, adj)
    x, adj = _rec_inputs()

    def _L0_gnn_setup():
        import jax, jax.numpy as jnp
        import numpy as np
        N = 2048
        D_IN = 512
        H = 16
        DH = D_IN // H
        ALPHA = 0.2
        MASK_VAL = -65500.0
        key = jax.random.key(seed)
        ks = jax.random.split(key, 7)
        x = jax.random.normal(ks[0], (N, D_IN), dtype=jnp.float32)
        adj = jax.random.randint(ks[1], (N, N), 0, 2).astype(jnp.float32)
        s = 1.0 / np.sqrt(D_IN)
        W_seq = jax.random.normal(ks[2], (D_IN, D_IN), dtype=jnp.float32) * s
        a1 = jax.random.normal(ks[3], (DH,), dtype=jnp.float32) / np.sqrt(DH)
        a2 = jax.random.normal(ks[4], (DH,), dtype=jnp.float32) / np.sqrt(DH)
        W_out = jax.random.normal(ks[5], (D_IN, D_IN), dtype=jnp.float32) * s
        b_out = jax.random.normal(ks[6], (D_IN,), dtype=jnp.float32) * 0.01
        return {'x': x, 'adj': adj, 'W_seq': W_seq, 'a1': a1, 'a2': a2, 'W_out': W_out, 'b_out': b_out}
    _L0_gnn_all = _L0_gnn_setup()
    _L0_gnn_in = {k: v for k, v in _L0_gnn_all.items() if k in ('W_seq', 'a1', 'a2', 'W_out', 'b_out')}
    del _L0_gnn_all

    def _L1_gnn_setup():
        import jax, jax.numpy as jnp
        import numpy as np
        N = 4096
        IN_FEATURES = 512
        OUT_FEATURES = 512
        key = jax.random.key(seed)
        k_x, k_adj, k_w, k_b = jax.random.split(key, 4)
        x = jax.random.normal(k_x, (N, IN_FEATURES), dtype=jnp.float32)
        adj = jax.random.uniform(k_adj, (N, N), dtype=jnp.float32)
        stdv = 1.0 / np.sqrt(OUT_FEATURES)
        weight = jax.random.uniform(k_w, (IN_FEATURES, OUT_FEATURES), dtype=jnp.float32, minval=-stdv, maxval=stdv)
        bias = jax.random.uniform(k_b, (OUT_FEATURES,), dtype=jnp.float32, minval=-stdv, maxval=stdv)
        return {'x': x, 'adj': adj, 'weight': weight, 'bias': bias}
    _L1_gnn_all = _L1_gnn_setup()
    _L1_gnn_in = {k: v for k, v in _L1_gnn_all.items() if k in ('weight', 'bias')}
    del _L1_gnn_all
    return {'x': x, 'adj': adj, 'L0_gnn_W_seq': _L0_gnn_in['W_seq'], 'L0_gnn_a1': _L0_gnn_in['a1'], 'L0_gnn_a2': _L0_gnn_in['a2'], 'L0_gnn_W_out': _L0_gnn_in['W_out'], 'L0_gnn_b_out': _L0_gnn_in['b_out'], 'L1_gnn_weight': _L1_gnn_in['weight'], 'L1_gnn_bias': _L1_gnn_in['bias']}

def reference(x, adj, L0_gnn_W_seq, L0_gnn_a1, L0_gnn_a2, L0_gnn_W_out, L0_gnn_b_out, L1_gnn_weight, L1_gnn_bias):
    import jax
    import jax.numpy as jnp

    def _L0_gnn_ref(x, adj, W_seq, a1, a2, W_out, b_out):
        import jax, jax.numpy as jnp
        import numpy as np
        N = 2048
        D_IN = 512
        H = 16
        DH = D_IN // H
        ALPHA = 0.2
        MASK_VAL = -65500.0
        seq = (x @ W_seq).reshape(N, H, DH)
        score1 = jnp.einsum('nhd,d->hn', seq, a1)
        score2 = jnp.einsum('nhd,d->hn', seq, a2)
        scores = score1[:, :, None] + score2[:, None, :]
        scores = jax.nn.leaky_relu(scores, negative_slope=ALPHA)
        scores = scores + (1.0 - adj)[None, :, :] * MASK_VAL
        attn = jax.nn.softmax(scores, axis=-1)
        hidden = jnp.einsum('hij,jhd->ihd', attn, seq).reshape(N, D_IN)
        hidden = hidden @ W_out + b_out
        return jax.nn.elu(hidden)

    def _L1_gnn_ref(x, adj, weight, bias):
        import jax, jax.numpy as jnp
        import numpy as np
        N = 4096
        IN_FEATURES = 512
        OUT_FEATURES = 512
        support = jnp.matmul(x, weight)
        output = jnp.matmul(adj, support)
        return output + bias
    x = _layernorm(x + _L0_gnn_ref(x, adj, L0_gnn_W_seq, L0_gnn_a1, L0_gnn_a2, L0_gnn_W_out, L0_gnn_b_out), axis=-1)
    x = _layernorm(x + _L1_gnn_ref(x, adj, L1_gnn_weight, L1_gnn_bias), axis=-1)
    return x

_drawn_inputs = setup_inputs


def setup_inputs(seed=0):
    import zlib

    import numpy as np

    out = dict(_drawn_inputs(seed))
    spreads = {}
    factors = {'L0_gnn_b_out': 3.896, 'L1_gnn_bias': 3.878}
    for name, (base, spread) in spreads.items():
        noise = np.random.default_rng([zlib.crc32(name.encode()), seed]).standard_normal(out[name].shape)
        drawn = base * np.exp(spread * noise) if base else spread * noise
        out[name] = jnp.asarray(drawn.astype(out[name].dtype))
    for name, factor in factors.items():
        out[name] = (out[name] * factor).astype(out[name].dtype)
    return out
```

```python
import concourse.bass as bass
from concourse import mybir
from contextlib import ExitStack

P = 128
N = 2048
D = 512
H = 16
DH = D // H
T = N // P
KC = D // P
HALVES = 2
TH = T // HALVES
NH = N // HALVES
C = DH + 1
CV = 2 * C
CW = 2 * CV
PAIRS = H // 2
CH = 4
NCH = T // CH
BANK = 512
TB = BANK // CW
AG = [(0, 6), (6, 11), (11, 16)]
SLOPE = 0.2
STEEP = 2.0 ** 40
UP = 64.0
FP8_ONE = 56
EPS = 1e-5

fp32, fp16, bf16 = mybir.dt.float32, mybir.dt.float16, mybir.dt.bfloat16
fp8, u8, u32 = mybir.dt.float8e4, mybir.dt.uint8, mybir.dt.uint32
ALU = mybir.AluOpType
ACT = mybir.ActivationFunctionType
AX = mybir.AxisListType


def spread(ap, shape):
    return ap.to_broadcast(shape)


def project_nodes(nc, x, adj, w, a1, a2, s1_rows, g_rows, adjT, hid, V, AB, S2):
    ctx = ExitStack()
    with ctx:
        def sb(name, shape, dt):
            return ctx.enter_context(nc.sbuf_tensor(name, shape, dt))

        def pb(name, shape, dt):
            return ctx.enter_context(nc.psum_tensor(name, shape, dt))

        def sem(name):
            return ctx.enter_context(nc.semaphore(name))

        WX = D + 2 * H
        xt = sb("xt", [P, 2, D], fp32)
        at = sb("at", [P, 2, N], fp32)
        ab = sb("ab", [P, 2, N], bf16)
        xh = sb("xh", [P, 2, KC, P], fp16)
        xl = sb("xl", [P, 2, KC, P], fp16)
        wf = sb("wf", [P, KC, WX], fp32)
        wp = sb("wp", [P, H, DH], fp32)
        wh = sb("wh", [P, KC, WX], fp16)
        wl = sb("wl", [P, KC, WX], fp16)
        av = sb("av", [P, 2, DH], fp32)
        seq = hid[:].rearrange("p t h c -> p (t h c)")[:, 0:T * D].rearrange("p (t d) -> p t d", t=T)
        sc = sb("sc", [P, T, 2, H], fp32)
        srow = at[0:2 * H, 0, :]
        gmx = sb("gmx", [2 * H, 1], fp32)
        G = sb("G", [P, H], fp32)
        tt = sb("tt", [P, T, H], fp32)
        lr = sb("lr", [P, T, H], fp32)
        ea = sb("ea", [P, 2, T, H], fp32)
        F = sb("F", [P, 2, T, H], fp32)
        vt = wf[:].rearrange("p k n -> p (k n)")[:, 0:2 * T * CV].rearrange("p (u t a c) -> p u t a c", u=2, t=T, a=2)
        idf = sb("idf", [P, P], fp32)
        idb = sb("idb", [P, P], bf16)
        pxt = [pb(f"pxt{u}", [P, KC, P], fp32) for u in range(2)]
        psq = [pb(f"psq{u}", [P, D], fp32) for u in range(2)]
        psc = [pb(f"psc{u}", [P, 2 * H], fp32) for u in range(2)]
        pat = [pb(f"pat{u}", [P, TH, P], bf16) for u in range(2)]

        w_loaded = sem("w_loaded")
        a_loaded = sem("a_loaded")
        x_loaded = [sem(f"x_loaded{u}") for u in range(2)]
        adj_loaded = [sem(f"adj_loaded{u}") for u in range(2)]
        ones_set = sem("ones_set")
        ident_ready = sem("ident_ready")
        w_step = sem("w_step")
        w_high = sem("w_high")
        w_split = sem("w_split")
        adj_cast = sem("adj_cast")
        x_turned = sem("x_turned")
        x_high = sem("x_high")
        x_split = sem("x_split")
        adj_turned = sem("adj_turned")
        adj_out = sem("adj_out")
        projected = sem("projected")
        seq_out = sem("seq_out")
        score_out = sem("score_out")
        score_turned = sem("score_turned")
        row_out = sem("row_out")
        row_max = sem("row_max")
        row_stored = sem("row_stored")
        g_stored = sem("g_stored")
        g_loaded = sem("g_loaded")
        e_step = sem("e_step")
        exp_in = sem("exp_in")
        exp_out = sem("exp_out")
        pos_scaled = sem("pos_scaled")
        neg_scaled = sem("neg_scaled")
        v_high = sem("v_high")
        v_split = sem("v_split")
        passed = sem("passed_a")

        block = ctx.enter_context(nc.Block())

        @block.sync
        def _(sp):
            sp.dma_start(wf[:, :, 0:D], w.rearrange("(k p) n -> p k n", p=P)).then_inc(w_loaded, 16)
            sp.dma_start(av[:, 0, :], a1[None, :].to_broadcast([P, DH])).then_inc(a_loaded, 16)
            sp.dma_start(av[:, 1, :], a2[None, :].to_broadcast([P, DH])).then_inc(a_loaded, 16)

            def load(t, u, first):
                if not first:
                    sp.wait_ge(x_turned, t - 1)
                sp.dma_start(xt[:, u, :], x[t, :, :]).then_inc(x_loaded[u], 16)
                if not first:
                    sp.wait_ge(adj_cast, t - 1)
                sp.dma_start(at[:, u, :], adj[t, :, :]).then_inc(adj_loaded[u], 16)

            for u in range(2):
                load(u, u, True)
            with sp.Fori(1, T // 2) as i:
                for u in range(2):
                    load(2 * i + u, u, False)
            sp.wait_ge(row_out, 4)
            sp.dma_start(s1_rows[:, :], srow[0:H, :]).then_inc(row_stored, 16)
            sp.wait_ge(row_max, 1)
            sp.dma_start(g_rows[:, :], gmx[H:2 * H, :]).then_inc(g_stored, 16)
            sp.wait_ge(g_stored, 16)
            sp.dma_start(G[:, :], g_rows.rearrange("h o -> o h").to_broadcast([P, H])).then_inc(g_loaded, 16)
            sp.wait_ge(row_stored, 16)

        @block.gpsimd
        def _(pool):
            nc.gpsimd.memset(idf[:], 1.0).then_inc(ones_set, 1)
            nc.gpsimd.memset(idb[:], 1.0).then_inc(ones_set, 1)
            pool.wait_ge(ones_set, 2)
            for m in (idf, idb):
                nc.gpsimd.affine_select(out=m[:], in_=m[:], compare_op=ALU.is_equal, fill=0.0, base=0,
                                        pattern=[[-1, P]], channel_multiplier=1).then_inc(ident_ready, 1)

            def cast(t, u, i, first):
                pool.wait_ge(adj_loaded[u], 16 * i + 16)
                if not first:
                    pool.wait_ge(adj_turned, 2 * t - 2).then_inc(passed, 1)
                nc.gpsimd.tensor_copy(ab[:, u, :], at[:, u, :]).then_inc(adj_cast, 1)

            for u in range(2):
                cast(u, u, 0, True)
            with pool.Fori(1, T // 2) as i:
                for u in range(2):
                    cast(2 * i + u, u, i, False)

            pool.wait_ge(exp_out, 2)
            pool.wait_ge(seq_out, T)

            def scale(h, u, first):
                if not first:
                    pool.wait_ge(v_split, h - 1)
                nc.gpsimd.tensor_tensor(vt[:, u, :, 0, 0:DH], seq[:, :, bass.ds(h * DH, DH)],
                                        spread(F[:, 0, :, bass.ds(h, 1)], [P, T, DH]), ALU.mult).then_inc(pos_scaled, 1)

            for u in range(2):
                scale(u, u, True)
            with pool.Fori(1, H // 2) as i:
                for u in range(2):
                    scale(2 * i + u, u, False)

        @block.scalar
        def _(act):
            act.wait_ge(w_step, 2 * KC)
            nc.scalar.activation(wh[:], wf[:], ACT.Copy, scale=UP).then_inc(w_high, 1)

            def evict_seq(t, u):
                act.wait_ge(projected, t + 1)
                nc.scalar.activation(seq[:, t, :], psq[u][:], ACT.Copy).then_inc(seq_out, 1)

            def slot(t, u, first, second):
                act.wait_ge(x_turned, t + 1)
                if not first and not second:
                    act.wait_ge(projected, t - 1)
                nc.scalar.activation(xh[:, u], pxt[u][:], ACT.Copy).then_inc(x_high, 1)
                for f in range(2):
                    act.wait_ge(adj_turned, 2 * t + f + 1)
                    nc.scalar.activation(adjT[:, t, f * TH:(f + 1) * TH, :], pat[f][:], ACT.Copy,
                                         scale=float(FP8_ONE)).then_inc(adj_out, 1)
                if not first:
                    evict_seq(t - 1, 1 - u)

            slot(0, 0, True, False)
            slot(1, 1, False, True)
            with act.Fori(1, T // 2) as i:
                for u in range(2):
                    slot(2 * i + u, u, False, False)
            evict_seq(T - 1, 1)

            act.wait_ge(adj_cast, T)
            for b in range(4):
                act.wait_ge(score_turned, b + 1)
                nc.scalar.activation(srow[:, b * BANK:(b + 1) * BANK], (psq + psc)[b][0:2 * H, :] if b < 2 else
                                     pxt[b - 2][0:2 * H].rearrange("h a b -> h (a b)"), ACT.Copy).then_inc(row_out, 1)
            act.wait_ge(exp_in, 1)
            nc.scalar.activation(F[:, 0], tt[:], ACT.Exp).then_inc(exp_out, 1)
            nc.scalar.activation(F[:, 1], tt[:], ACT.Exp, scale=SLOPE).then_inc(exp_out, 1)
            act.wait_ge(e_step, 4)
            nc.scalar.activation(ea[:], ea[:], ACT.Exp).then_inc(exp_out, 1)

            def high(h, u):
                act.wait_ge(pos_scaled, h + 1)
                act.wait_ge(neg_scaled, 2 * h + 2)
                nc.scalar.activation(V[:, h, :, 0:CV], vt[:, u].rearrange("p t a c -> p t (a c)"),
                                     ACT.Copy).then_inc(v_high, 1)

            with act.Fori(0, H // 2) as i:
                for u in range(2):
                    high(2 * i + u, u)

        @block.vector
        def _(dve):
            dve.wait_ge(w_loaded, 16)
            dve.wait_ge(a_loaded, 32)
            for k in range(KC):
                for s in range(2):
                    if k or s:
                        dve.wait_ge(w_step, 2 * k + s)
                    nc.vector.tensor_tensor(wp[:], wf[:, k, 0:D].rearrange("p (h d) -> p h d", h=H),
                                            spread(av[:, s:s + 1, :], [P, H, DH]), ALU.mult).then_inc(score_out, 1)
                    dve.wait_ge(score_out, 2 * k + s + 1)
                    nc.vector.tensor_reduce(wf[:, k, D + s * H:D + (s + 1) * H], wp[:], AX.X,
                                            ALU.add).then_inc(w_step, 1)
            dve.wait_ge(w_high, 1)
            nc.vector.scalar_tensor_tensor(wl[:], wf[:], UP, wh[:], ALU.mult, ALU.subtract).then_inc(w_split, 1)
            scored = 2 * KC

            def evict_scores(t, u):
                dve.wait_ge(projected, t + 1)
                nc.vector.tensor_scalar(sc[:, t].rearrange("p s h -> p (s h)"), psc[u][:], 1.0 / UP, None,
                                        ALU.mult).then_inc(score_out, 1)

            def slot(t, u, first):
                dve.wait_ge(x_high, t + 1)
                nc.vector.tensor_tensor(xl[:, u], pxt[u][:], xh[:, u], ALU.subtract).then_inc(x_split, 1)
                if not first:
                    evict_scores(t - 1, 1 - u)

            slot(0, 0, True)
            slot(1, 1, False)
            with dve.Fori(1, T // 2) as i:
                for u in range(2):
                    slot(2 * i + u, u, False)
            evict_scores(T - 1, 1)

            dve.wait_ge(score_out, scored + T)
            nc.vector.tensor_scalar(S2[:, :, 0, :], sc[:, :, 1, :].rearrange("p t h -> p h t"), -1.0, None, ALU.mult)
            nc.vector.tensor_scalar(S2[:, :, 1, :], sc[:, :, 1, :].rearrange("p t h -> p h t"), STEEP, None, ALU.mult)
            dve.wait_ge(row_out, 4)
            nc.vector.tensor_reduce(gmx[:], srow, AX.X, ALU.max).then_inc(row_max, 1)
            dve.wait_ge(g_loaded, 16)
            g = spread(G[:, None, :], [P, T, H])
            nc.vector.tensor_tensor(tt[:], sc[:, :, 1, :], g, ALU.subtract).then_inc(exp_in, 1)
            dve.wait_ge(exp_out, 2)
            nc.vector.tensor_tensor(tt[:], sc[:, :, 0, :], g, ALU.add).then_inc(e_step, 1)
            dve.wait_ge(e_step, 1)
            nc.vector.scalar_tensor_tensor(lr[:], tt[:], SLOPE, tt[:], ALU.mult, ALU.max).then_inc(e_step, 1)
            dve.wait_ge(e_step, 2)
            nc.vector.tensor_tensor(ea[:, 0], tt[:], lr[:], ALU.subtract).then_inc(e_step, 1)
            nc.vector.scalar_tensor_tensor(ea[:, 1], tt[:], SLOPE, lr[:], ALU.mult, ALU.subtract).then_inc(e_step, 1)
            dve.wait_ge(exp_out, 3)
            nc.vector.tensor_scalar(AB[:, :, 0, :], ea[:, 0], 1.0, None, ALU.mult)
            nc.vector.tensor_scalar(AB[:, :, 1, :], ea[:, 1], -1.0, None, ALU.mult)
            dve.wait_ge(seq_out, T)

            def weigh(h, u, first):
                if not first:
                    dve.wait_ge(v_split, h - 1)
                nc.vector.tensor_tensor(vt[:, u, :, 1, 0:DH], seq[:, :, bass.ds(h * DH, DH)],
                                        spread(F[:, 1, :, bass.ds(h, 1)], [P, T, DH]), ALU.mult).then_inc(neg_scaled, 1)
                nc.vector.tensor_scalar(vt[:, u, :, :, DH].rearrange("p t a -> p a t"), F[:, :, :, h], UP, None,
                                        ALU.mult).then_inc(neg_scaled, 1)

            def low(h, u):
                dve.wait_ge(v_high, h + 1)
                nc.vector.tensor_tensor(V[:, h, :, CV:CW], vt[:, u].rearrange("p t a c -> p t (a c)"),
                                        V[:, h, :, 0:CV], ALU.subtract).then_inc(v_split, 1)

            weigh(0, 0, True)
            weigh(1, 1, True)
            low(0, 0)
            with dve.Fori(1, H // 2) as i:
                for u in range(2):
                    weigh(2 * i + u, u, False)
                    low(2 * i + u - 1, 1 - u)
            low(H - 1, 1)

        @block.tensor
        def _(pe):
            pe.wait_ge(ident_ready, 2)

            def slot(t, u, i, first, very_first):
                pe.wait_ge(x_loaded[u], 16 * i + 16)
                if not first:
                    pe.wait_ge(x_split, t - 1)
                for k in range(KC):
                    last = nc.tensor.transpose(pxt[u][:, k, :], xt[:, u, k * P:(k + 1) * P], idf[:])
                last.then_inc(x_turned, 1)
                pe.wait_ge(adj_cast, t + 1)
                for f in range(2):
                    if not very_first:
                        pe.wait_ge(adj_out, 2 * t + f - 1)
                    for b in range(TH):
                        c = (f * TH + b) * P
                        last = nc.tensor.transpose(pat[f][:, b, :], ab[:, u, c:c + P], idb[:])
                    last.then_inc(adj_turned, 1)
                pe.wait_ge(x_split, t + 1)
                if very_first:
                    pe.wait_ge(w_split, 1)
                if not first:
                    pe.wait_ge(seq_out, t - 1)
                    pe.wait_ge(score_out, 2 * KC + t - 1)
                for k in range(KC):
                    for m, (lhs, rhs) in enumerate(((xh, wh), (xh, wl), (xl, wh))):
                        st, en = k == 0 and m == 0, k == KC - 1 and m == 2
                        nc.tensor.matmul(psq[u][:], lhs[:, u, k, :], rhs[:, k, 0:D], start=st, stop=en)
                        last = nc.tensor.matmul(psc[u][:], lhs[:, u, k, :], rhs[:, k, D:WX], start=st, stop=en)
                last.then_inc(projected, 1)

            slot(0, 0, 0, True, True)
            slot(1, 1, 0, True, False)
            with pe.Fori(1, T // 2) as i:
                for u in range(2):
                    slot(2 * i + u, u, i, False, False)
            pe.wait_ge(score_out, 2 * KC + T)
            pe.wait_ge(seq_out, T)
            for t in range(T):
                bank = (psq[0][0:2 * H, :], psq[1][0:2 * H, :], pxt[0][0:2 * H].rearrange("h a b -> h (a b)"),
                        pxt[1][0:2 * H].rearrange("h a b -> h (a b)"))[t // 4]
                ins = nc.tensor.transpose(bank[:, (t % 4) * P:(t % 4 + 1) * P],
                                          sc[:, t].rearrange("p s h -> p (s h)"), idf[:])
                if t % 4 == 3:
                    ins.then_inc(score_turned, 1)


def attend(nc, s1_rows, adjT, V, AB, S2, hid):
    ctx = ExitStack()
    with ctx:
        def sb(name, shape, dt):
            return ctx.enter_context(nc.sbuf_tensor(name, shape, dt))

        def pb(name, shape, dt):
            return ctx.enter_context(nc.psum_tensor(name, shape, dt))

        def sem(name):
            return ctx.enter_context(nc.semaphore(name))

        edge = [sb(f"edge{a}", [P, T, NH], u8) for a in range(2)]
        vcur = [sb(f"vcur{a}", [P, T, CW], fp16) for a in range(2)]
        s1b = [sb(f"s1b{a}", [P, NH], fp32) for a in range(2)]
        s2c = [sb(f"s2c{a}", [P, 2, T], fp32) for a in range(2)]
        tile = sb("tile", [P, T, P], u8)
        esum = [sb(f"esum{a}", [P, TH, CW], fp32) for a in range(2)]
        asum = sb("asum", [P, H, CV], fp32)
        pair = sb("pair", [P, TH, 2, C], fp32)
        plain = sb("plain", [P, H, C], fp32)
        pe_e = [pb(f"pe_e{a}", [P, 3, BANK], fp32) for a in range(2)]
        pe_a = [pb(f"pe_a{b}", [P, BANK], fp32) for b in range(2)]

        head_in = [sem(f"head_in{a}") for a in range(2)]
        v_in = [sem(f"v_in{a}") for a in range(2)]
        tile_in = sem("tile_in")
        act_passed = sem("act_passed")
        pe_passed = sem("pe_passed")
        pool_passed = sem("pool_passed")
        act_sign = sem("act_sign")
        dve_sign = sem("dve_sign")
        masked = sem("masked")
        head_done = sem("head_done")
        plain_done = sem("plain_done")
        head_out = sem("head_out")
        plain_out = sem("plain_out")
        joined = sem("joined")
        joined_a = sem("joined_a")
        p_step = sem("p_step")
        q_step = sem("q_step")
        cleared = sem("cleared")

        ITER = HALVES * PAIRS
        assert ITER == T
        block = ctx.enter_context(nc.Block())

        @block.sync
        def _(sp):
            def load(it, half, p, first):
                for a in range(2):
                    g = 2 * it + a
                    if not first:
                        sp.wait_ge(masked, NCH * (g - 1))
                    sp.dma_start(s1b[a][:], s1_rows[bass.ds(2 * p + a, 1), bass.ds(half * NH, NH)]
                                 .to_broadcast([P, NH])).then_inc(head_in[a], 16)
                    sp.dma_start(s2c[a][:], S2[:, 2 * p + a, :, :]).then_inc(head_in[a], 16)
                    if not first:
                        sp.wait_ge(head_done, g - 1)
                    sp.dma_start(vcur[a][:], V[:, 2 * p + a, :, :]).then_inc(v_in[a], 16)
                    if a == 0:
                        if not first:
                            sp.wait_ge(plain_done, 3 * it)
                        sp.dma_start(tile[:], adjT[:, it, :, :]).then_inc(tile_in, 16)

            load(0, 0, 0, True)
            with sp.Fori(1, PAIRS) as p:
                load(p, 0, p, False)
            with sp.Fori(0, PAIRS) as p:
                load(p + PAIRS, 1, p, False)

        @block.scalar
        def _(act):
            def evict(g, a, first):
                act.wait_ge(head_done, g + 1)
                if not first:
                    act.wait_ge(joined, g - 1)
                nc.scalar.activation(esum[a][:, 0:2 * TB, :].rearrange("p (b t) c -> p b (t c)", b=2),
                                     pe_e[a][:, 0:2, 0:TB * CW], ACT.Copy).then_inc(head_out, 1)
                nc.scalar.activation(esum[a][:, 2 * TB:TH, :].rearrange("p t c -> p (t c)"),
                                     pe_e[a][:, 2, 0:(TH - 2 * TB) * CW], ACT.Copy).then_inc(head_out, 1)

            def slots(it, first):
                for a in range(2):
                    g = 2 * it + a
                    act.wait_ge(head_in[a], 32 * it + 32)
                    if not first:
                        act.wait_ge(head_done, g - 1).then_inc(act_passed, 1)
                    for c in range(NCH):
                        for j in range(CH * c + CH // 2, CH * (c + 1)):
                            ins = nc.scalar.activation(edge[a][:, j, :].bitcast(fp8), s1b[a][:], ACT.Sigmoid,
                                                       bias=s2c[a][:, 1, j:j + 1], scale=STEEP, saturate=False)
                        ins.then_inc(act_sign, 1)
                    if not (first and a == 0):
                        evict(g - 1, 1 - a, first)

            slots(0, True)
            with act.Fori(1, ITER) as it:
                slots(it, False)
            evict(2 * ITER - 1, 1, False)

        @block.vector
        def _(dve):
            def evict_plain(n, k):
                h0, h1 = AG[k]
                dve.wait_ge(plain_done, n + 1)
                nc.vector.tensor_copy(asum[:, h0:h1, :].rearrange("p h c -> p (h c)"),
                                      pe_a[k % 2][:, 0:(h1 - h0) * CV]).then_inc(plain_out, 1)

            def slots(it, half, first):
                for a in range(2):
                    g = 2 * it + a
                    dve.wait_ge(head_in[a], 32 * it + 32)
                    if not first:
                        dve.wait_ge(head_done, g - 1)

                    def sign(c):
                        for j in range(CH * c, CH * c + CH // 2):
                            ins = nc.vector.tensor_scalar(edge[a][:, j, :], s1b[a][:], s2c[a][:, 0, j:j + 1],
                                                          float(FP8_ONE), ALU.is_gt, ALU.mult)
                        ins.then_inc(dve_sign, 1)

                    sign(0)
                    for c in range(NCH):
                        if c + 1 < NCH:
                            sign(c + 1)
                        dve.wait_ge(act_sign, NCH * g + c + 1)
                        dve.wait_ge(dve_sign, NCH * g + c + 1)
                        e = edge[a][:, CH * c:CH * (c + 1), :].rearrange("p j (t i) -> p j t i", t=TH).bitcast(u32)
                        m = adjT[:, half * TH:(half + 1) * TH, CH * c:CH * (c + 1), :].rearrange(
                            "p t j i -> p j t i").bitcast(u32)
                        nc.vector.tensor_tensor(e, e, m, ALU.bitwise_and).then_inc(masked, 1)
                    if a == 1:
                        if not first:
                            dve.wait_ge(joined_a, it)
                        evict_plain(3 * it, 0)
                    elif not first:
                        evict_plain(3 * it - 2, 1)
                        evict_plain(3 * it - 1, 2)

            slots(0, 0, True)
            with dve.Fori(1, PAIRS) as p:
                slots(p, 0, False)
            with dve.Fori(0, PAIRS) as p:
                slots(p + PAIRS, 1, False)
            evict_plain(3 * ITER - 2, 1)
            evict_plain(3 * ITER - 1, 2)

        @block.tensor
        def _(pe):
            def plain_sum(it, k, first):
                h0, h1 = AG[k]
                if k == 2 or not first:
                    pe.wait_ge(plain_out, 3 * it + (0, -1, 1)[k]).then_inc(pe_passed, 1)
                if k == 0:
                    pe.wait_ge(tile_in, 16 * it + 16).then_inc(pe_passed, 1)
                for j in range(T):
                    ins = nc.tensor.matmul(pe_a[k % 2][:, 0:(h1 - h0) * CV], tile[:, j, :].bitcast(fp8),
                                           V[:, h0:h1, j, :].rearrange("p h (w c) -> p h w c", w=2)[:, :, :, C:CV],
                                           start=(j == 0), stop=(j == T - 1))
                ins.then_inc(plain_done, 1)

            def slots(it, first):
                for a in range(2):
                    g = 2 * it + a
                    pe.wait_ge(v_in[a], 16 * it + 16)
                    if not first:
                        pe.wait_ge(head_out, 2 * g - 2)
                    for c in range(NCH):
                        pe.wait_ge(masked, NCH * g + c + 1).then_inc(pe_passed, 1)
                        for j in range(CH * c, CH * (c + 1)):
                            for i in range(TH):
                                b, o = i // TB, (i % TB) * CW
                                ins = nc.tensor.matmul(pe_e[a][:, b, o:o + CW],
                                                       edge[a][:, j, i * P:(i + 1) * P].bitcast(fp8), vcur[a][:, j, :],
                                                       start=(j == 0 and i % TB == 0), stop=(j == T - 1),
                                                       skip_group_check=True)
                    ins.then_inc(head_done, 1)
                    for k in ((0,), (1, 2))[a]:
                        plain_sum(it, k, first)

            slots(0, True)
            with pe.Fori(1, ITER) as it:
                slots(it, False)

        @block.gpsimd
        def _(pool):
            nc.gpsimd.memset(hid[:], 0.0).then_inc(cleared, 1)
            pool.wait_ge(cleared, 1)

            def join(g, half, h, a):
                pool.wait_ge(head_out, 2 * g + 2)
                nc.gpsimd.tensor_tensor(pair[:].rearrange("p t s c -> p t (s c)"), esum[a][:, :, 0:CV],
                                        esum[a][:, :, CV:CW], ALU.add).then_inc(joined, 1)
                pool.wait_ge(joined, g + 1).then_inc(pool_passed, 1)
                nc.gpsimd.tensor_tensor(pair[:], pair[:],
                                        spread(AB[:, half * TH:(half + 1) * TH, :, bass.ds(h, 1)],
                                               [P, TH, 2, C]), ALU.mult).then_inc(p_step, 1)
                for s in range(2):
                    pool.wait_ge(p_step, 3 * g + s + 1).then_inc(pool_passed, 1)
                    nc.gpsimd.tensor_tensor(hid[:, half * TH:(half + 1) * TH, h, :],
                                            hid[:, half * TH:(half + 1) * TH, h, :], pair[:, :, s, :],
                                            ALU.add).then_inc(p_step, 1)
                pool.wait_ge(p_step, 3 * g + 3)

            def join_plain(t):
                pool.wait_ge(plain_out, 3 * t + 3)
                nc.gpsimd.tensor_tensor(plain[:], asum[:, :, 0:C], asum[:, :, C:CV], ALU.add).then_inc(joined_a, 1)
                pool.wait_ge(joined_a, t + 1).then_inc(pool_passed, 1)
                nc.gpsimd.tensor_tensor(plain[:], plain[:], spread(AB[:, t, 1, :][:, :, None], [P, H, C]),
                                        ALU.mult).then_inc(q_step, 1)
                pool.wait_ge(q_step, 2 * t + 1).then_inc(pool_passed, 1)
                nc.gpsimd.tensor_tensor(hid[:, t], hid[:, t], plain[:], ALU.subtract).then_inc(q_step, 1)
                pool.wait_ge(q_step, 2 * t + 2)

            join(0, 0, 0, 0)
            with pool.Fori(1, PAIRS) as p:
                join(2 * p - 1, 0, 2 * p - 1, 1)
                join_plain(p - 1)
                join(2 * p, 0, 2 * p, 0)
            join(H - 1, 0, H - 1, 1)
            join_plain(PAIRS - 1)
            join(H, 1, 0, 0)
            with pool.Fori(1, PAIRS) as p:
                join(H + 2 * p - 1, 1, 2 * p - 1, 1)
                join_plain(PAIRS + p - 1)
                join(H + 2 * p, 1, 2 * p, 0)
            join(2 * H - 1, 1, H - 1, 1)
            join_plain(T - 1)


def finish(nc, x, w_out, b_out, w1, b1, out, adjT, hid):
    ctx = ExitStack()
    with ctx:
        def sb(name, shape, dt):
            return ctx.enter_context(nc.sbuf_tensor(name, shape, dt))

        def pb(name, shape, dt):
            return ctx.enter_context(nc.psum_tensor(name, shape, dt))

        def sem(name):
            return ctx.enter_context(nc.semaphore(name))

        wf = [sb(f"wf{m}", [P, KC, D], fp32) for m in range(2)]
        wh = [sb(f"wh_{m}", [P, KC, D], fp16) for m in range(2)]
        wl = [sb(f"wl_{m}", [P, KC, D], fp16) for m in range(2)]
        bias = sb("bias", [P, 2, D], fp32)
        idf = sb("idf2", [P, P], fp32)
        xr = sb("xr", [P, 2, D], fp32)
        rec = sb("rec", [P, T, H], fp32)
        ht = sb("ht", [P, 2, D], fp32)
        th = sb("th", [P, 2, KC, P], fp16)
        tl = sb("tl", [P, 2, KC, P], fp16)
        y = sb("y", [P, 2, D], fp32)
        yr = sb("yr", [P, 2, D], fp32)
        ye = sb("ye", [P, 2, D], fp32)
        z = sb("z", [P, 2, D], fp32)
        st = sb("st", [P, 2, 6], fp32)
        mv = sb("mv", [P, 2, 2], fp32)
        ve = sb("ve", [P, 2, 1], fp32)
        rs = sb("rs", [P, 2, 1], fp32)
        consts = sb("consts", [P, 2], fp32)
        x1 = sb("x1", [P, T, D], fp32)
        sh = sb("sh", [P, T, D], fp16)
        sl = sb("sl", [P, T, D], fp16)
        tile = [sb(f"tile_{u}", [P, T, P], u8) for u in range(2)]
        pt = [pb(f"pt{u}", [P, KC, P], fp32) for u in range(2)]
        pm = [pb(f"pm{u}", [P, D], fp32) for u in range(2)]
        po = [pb(f"po{u}", [P, D], fp32) for u in range(2)]

        w_in = sem("w_in")
        b_in = sem("b_in")
        ones_set = sem("ones_set2")
        ident_ready = sem("ident2")
        w_high = sem("w_high2")
        w_split = sem("w_split2")
        x_in = [sem(f"x_in{u}") for u in range(2)]
        tile_in = [sem(f"tile_in{u}") for u in range(2)]
        rec_ready = sem("rec_ready")
        hid_ready = sem("hid_ready")
        turned = sem("turned")
        t_high = sem("t_high")
        t_split = sem("t_split")
        mixed = sem("mixed")
        y_ready = sem("y_ready")
        y_neg = sem("y_neg")
        y_exp = sem("y_exp")
        y_elu = sem("y_elu")
        z_ready = sem("z_ready")
        stats_ready = sem("stats_ready")
        var_ready = sem("var_ready")
        eps_added = sem("eps_added")
        rstd_ready = sem("rstd_ready")
        x1_ready = sem("x1_ready")
        s_high = sem("s_high")
        s_split = sem("s_split")
        gathered = sem("gathered")
        y_pos = sem("y_pos")
        dve_passed = sem("dve_passed")
        pe_passed = sem("pe_passed2")
        pool_passed = sem("pool_passed2")
        o_step = sem("o_step")
        o_ready = sem("o_ready")
        stored = [sem(f"stored{u}") for u in range(2)]

        def over_tiles(eng, slot, ahead=None):
            for u in range(2):
                slot(u, u, 0, True)
                if ahead:
                    ahead(u + 1, 1 - u)
            end = T // 2 - (1 if ahead else 0)
            with eng.Fori(1, end) as i:
                for u in range(2):
                    slot(2 * i + u, u, i, False)
                    if ahead:
                        ahead(2 * i + u + 1, 1 - u)
            if ahead:
                slot(T - 2, 0, T // 2 - 1, False)
                ahead(T - 1, 1)
                slot(T - 1, 1, T // 2 - 1, False)

        block = ctx.enter_context(nc.Block())

        @block.sync
        def _(sp):
            for m, src in enumerate((w_out, w1)):
                sp.dma_start(wf[m][:], src.rearrange("(k p) n -> p k n", p=P)).then_inc(w_in, 16)
            for m, src in enumerate((b_out, b1)):
                sp.dma_start(bias[:, m, :], src[None, :].to_broadcast([P, D])).then_inc(b_in, 16)

            def load(t, u, i, first):
                if not first:
                    sp.wait_ge(z_ready, t - 1)
                sp.dma_start(xr[:, u, :], x[t, :, :]).then_inc(x_in[u], 16)

            over_tiles(sp, load)

            def edges(t, u, i, first):
                if not first:
                    sp.wait_ge(gathered, t - 1)
                sp.dma_start(tile[u][:], adjT[:, t, :, :]).then_inc(tile_in[u], 16)
                
            over_tiles(sp, edges)

        @block.gpsimd
        def _(pool):
            nc.gpsimd.memset(idf[:], 1.0).then_inc(ones_set, 1)
            nc.gpsimd.memset(consts[:, 0:1], EPS).then_inc(ones_set, 1)
            nc.gpsimd.memset(consts[:, 1:2], -0.5).then_inc(ones_set, 1)
            pool.wait_ge(ones_set, 3)
            nc.gpsimd.affine_select(out=idf[:], in_=idf[:], compare_op=ALU.is_equal, fill=0.0, base=0,
                                    pattern=[[-1, P]], channel_multiplier=1).then_inc(ident_ready, 1)
            pool.wait_ge(rec_ready, 1)

            def normalise(t, u):
                nc.gpsimd.tensor_tensor(ht[:, u, :].rearrange("p (h d) -> p h d", h=H), hid[:, t, :, 0:DH],
                                        spread(rec[:, t, :][:, :, None], [P, H, DH]), ALU.mult).then_inc(hid_ready, 1)

            def rstd(n, t, u):
                pool.wait_ge(var_ready, n + t + 1)
                nc.gpsimd.tensor_tensor(ve[:, u], mv[:, u, 1:2], consts[:, 0:1], ALU.add).then_inc(eps_added, 1)
                pool.wait_ge(eps_added, n + t + 1)
                nc.gpsimd.tensor_tensor(rs[:, u], ve[:, u], consts[:, 1:2], ALU.pow).then_inc(rstd_ready, 1)

            def residual(t, u, i, first):
                pool.wait_ge(x_in[u], 16 * i + 16)
                if not first:
                    pool.wait_ge(x1_ready, t - 1)
                pool.wait_ge(y_elu, t + 1)
                nc.gpsimd.tensor_tensor(z[:, u], ye[:, u], xr[:, u], ALU.add).then_inc(z_ready, 1)
                rstd(0, t, u)

            def slot(t, u, i, first):
                pool.wait_ge(turned, t + 1)
                normalise(t + 2, u)
                residual(t, u, i, first)

            for u in range(2):
                normalise(u, u)
            for u in range(2):
                slot(u, u, 0, True)
            with pool.Fori(1, T // 2 - 1) as i:
                for u in range(2):
                    slot(2 * i + u, u, i, False)
            for u in range(2):
                residual(T - 2 + u, u, T // 2 - 1, False)

            def again(t, u, i, first):
                pool.wait_ge(x1_ready, t + 1)
                pool.wait_ge(turned, T + t - 1).then_inc(pool_passed, 1)
                nc.gpsimd.tensor_copy(ht[:, u, :], x1[:, t, :]).then_inc(hid_ready, 1)

            over_tiles(pool, again)

            def second_residual(t, u, i, first):
                pool.wait_ge(o_step, t + 1)
                if not first:
                    pool.wait_ge(o_ready, t - 1)
                nc.gpsimd.tensor_tensor(z[:, u], ye[:, u], x1[:, t, :], ALU.add).then_inc(z_ready, 1)
                rstd(T, t, u)

            over_tiles(pool, second_residual)

        @block.scalar
        def _(act):
            for m in range(2):
                act.wait_ge(w_in, 32)
                nc.scalar.activation(wh[m][:], wf[m][:], ACT.Copy, scale=UP).then_inc(w_high, 1)

            def high(n, t, u, first):
                act.wait_ge(turned, n + t + 1)
                if not first:
                    act.wait_ge(mixed, n + t - 1)
                nc.scalar.activation(th[:, u], pt[u][:], ACT.Copy).then_inc(t_high, 1)

            def elu(t, u, i, first):
                act.wait_ge(y_ready, t + 1)
                nc.scalar.activation(yr[:, u], y[:, u], ACT.Relu, scale=-1.0).then_inc(y_neg, 1)
                act.wait_ge(y_neg, t + 1)
                if not first:
                    act.wait_ge(z_ready, t - 1)
                nc.scalar.activation(ye[:, u], yr[:, u], ACT.Exp, scale=-1.0).then_inc(y_exp, 1)

            high(0, 0, 0, True)
            high(0, 1, 1, True)
            elu(0, 0, 0, True)
            high(0, 2, 0, False)
            elu(1, 1, 0, True)
            with act.Fori(1, T // 2 - 1) as i:
                for u in range(2):
                    high(0, 2 * i + u + 1, 1 - u, False)
                    elu(2 * i + u, u, i, False)
            high(0, T - 1, 1, False)
            elu(T - 2, 0, T // 2 - 1, False)
            elu(T - 1, 1, T // 2 - 1, False)

            def s_out(t, u, i, first):
                act.wait_ge(mixed, T + t + 1)
                nc.scalar.activation(sh[:, t, :], pm[u][:], ACT.Copy).then_inc(s_high, 1)

            high(T, 0, 0, False)
            with act.Fori(0, T // 2 - 1) as i:
                for u in range(2):
                    high(T, 2 * i + u + 1, 1 - u, False)
                    s_out(2 * i + u, u, i, False)
            high(T, T - 1, 1, False)
            s_out(T - 2, 0, 0, False)
            s_out(T - 1, 1, 0, False)

            def store(t, u, i, first):
                act.wait_ge(o_ready, t + 1)
                act.dma_start(out[t, :, :], y[:, u]).then_inc(stored[u], 16)

            over_tiles(act, store)
            for u in range(2):
                act.wait_ge(stored[u], 16 * (T // 2))

        @block.vector
        def _(dve):
            nc.vector.reciprocal(rec[:], hid[:, :, :, DH]).then_inc(rec_ready, 1)
            for m in range(2):
                dve.wait_ge(w_high, m + 1)
                nc.vector.scalar_tensor_tensor(wl[m][:], wf[m][:], UP, wh[m][:], ALU.mult,
                                               ALU.subtract).then_inc(w_split, 1)
            dve.wait_ge(b_in, 32)

            def low(n, t, u):
                dve.wait_ge(t_high, n + t + 1)
                nc.vector.tensor_tensor(tl[:, u], pt[u][:], th[:, u], ALU.subtract).then_inc(t_split, 1)

            def norm(n, t, u, dst, ready):
                dve.wait_ge(z_ready, n + t + 1)
                nc.vector.bn_stats(st[:, u], z[:, u]).then_inc(stats_ready, 1)
                dve.wait_ge(stats_ready, n + t + 1).then_inc(dve_passed, 1)
                nc.vector.bn_aggr(mv[:, u], st[:, u]).then_inc(var_ready, 1)
                dve.wait_ge(rstd_ready, n + t + 1)
                nc.vector.tensor_scalar(dst, z[:, u], mv[:, u, 0:1], rs[:, u], ALU.subtract,
                                        ALU.mult).then_inc(ready, 1)

            def biased(t, u, first):
                dve.wait_ge(mixed, t + 1)
                if not first:
                    dve.wait_ge(y_elu, t - 1)
                nc.vector.scalar_tensor_tensor(y[:, u], pm[u][:], 1.0 / UP, bias[:, 0, :], ALU.mult,
                                               ALU.add).then_inc(y_ready, 1)

            def elu(t, u):
                dve.wait_ge(y_exp, t + 1)
                nc.vector.tensor_scalar(y[:, u], y[:, u], 0.0, -1.0, ALU.max, ALU.add).then_inc(y_pos, 1)
                dve.wait_ge(y_pos, t + 1)
                nc.vector.tensor_tensor(ye[:, u], y[:, u], ye[:, u], ALU.add).then_inc(y_elu, 1)

            low(0, 0, 0)
            low(0, 1, 1)
            biased(0, 0, True)
            elu(0, 0)
            low(0, 2, 0)
            biased(1, 1, True)
            elu(1, 1)
            norm(0, 0, 0, x1[:, 0, :], x1_ready)
            with dve.Fori(1, T // 2 - 1) as i:
                for u in range(2):
                    t = 2 * i + u
                    low(0, t + 1, 1 - u)
                    biased(t, u, False)
                    elu(t, u)
                    norm(0, t - 1, 1 - u, x1[:, t - 1, :], x1_ready)
            low(0, T - 1, 1)
            for t in (T - 2, T - 1):
                biased(t, t % 2, False)
                elu(t, t % 2)
                norm(0, t - 1, 1 - t % 2, x1[:, t - 1, :], x1_ready)
            norm(0, T - 1, 1, x1[:, T - 1, :], x1_ready)

            def s_low(t, u):
                dve.wait_ge(s_high, t + 1)
                nc.vector.tensor_tensor(sl[:, t, :], pm[u][:], sh[:, t, :], ALU.subtract).then_inc(s_split, 1)

            low(T, 0, 0)
            with dve.Fori(0, T // 2 - 1) as i:
                for u in range(2):
                    low(T, 2 * i + u + 1, 1 - u)
                    s_low(2 * i + u, u)
            low(T, T - 1, 1)
            s_low(T - 2, 0)
            s_low(T - 1, 1)

            def second(t, u, first):
                dve.wait_ge(gathered, t + 1)
                if not first:
                    dve.wait_ge(z_ready, T + t - 1)
                nc.vector.scalar_tensor_tensor(ye[:, u], po[u][:], 1.0 / UP, bias[:, 1, :], ALU.mult,
                                               ALU.add).then_inc(o_step, 1)

            def normed(t, u, i, first):
                if not first:
                    dve.wait_ge(stored[u], 16 * i)
                norm(T, t, u, y[:, u], o_ready)

            second(0, 0, True)
            second(1, 1, True)
            normed(0, 0, 0, True)
            second(2, 0, False)
            normed(1, 1, 0, True)
            with dve.Fori(1, T // 2 - 1) as i:
                for u in range(2):
                    second(2 * i + u + 1, 1 - u, False)
                    normed(2 * i + u, u, i, False)
            second(T - 1, 1, False)
            normed(T - 2, 0, T // 2 - 1, False)
            normed(T - 1, 1, T // 2 - 1, False)

        @block.tensor
        def _(pe):
            pe.wait_ge(ident_ready, 1)

            def turn(n, t, u, first):
                pe.wait_ge(hid_ready, n + t + 1)
                if not first:
                    pe.wait_ge(t_split, n + t - 1)
                for k in range(KC):
                    last = nc.tensor.transpose(pt[u][:, k, :], ht[:, u, k * P:(k + 1) * P], idf[:])
                last.then_inc(turned, 1)

            def mix(n, t, u, m, free, first):
                pe.wait_ge(t_split, n + t + 1)
                if not first:
                    pe.wait_ge(free, t - 1)
                for k in range(KC):
                    for q, (lhs, rhs) in enumerate(((th, wh[m]), (th, wl[m]), (tl, wh[m]))):
                        last = nc.tensor.matmul(pm[u][:], lhs[:, u, k, :], rhs[:, k, :],
                                                start=(k == 0 and q == 0), stop=(k == KC - 1 and q == 2))
                last.then_inc(mixed, 1)

            turn(0, 0, 0, True)
            turn(0, 1, 1, True)
            pe.wait_ge(w_split, 2)
            mix(0, 0, 0, 0, y_ready, True)
            turn(0, 2, 0, False)
            mix(0, 1, 1, 0, y_ready, True)
            with pe.Fori(1, T // 2 - 1) as i:
                for u in range(2):
                    turn(0, 2 * i + u + 1, 1 - u, False)
                    mix(0, 2 * i + u, u, 0, y_ready, False)
            turn(0, T - 1, 1, False)
            mix(0, T - 2, 0, 0, y_ready, False)
            mix(0, T - 1, 1, 0, y_ready, False)

            pe.wait_ge(y_ready, T)
            turn(T, 0, 0, False)
            turn(T, 1, 1, False)
            mix(T, 0, 0, 1, s_split, True)
            turn(T, 2, 0, False)
            mix(T, 1, 1, 1, s_split, True)
            with pe.Fori(1, T // 2 - 1) as i:
                for u in range(2):
                    turn(T, 2 * i + u + 1, 1 - u, False)
                    mix(T, 2 * i + u, u, 1, s_split, False)
            turn(T, T - 1, 1, False)
            mix(T, T - 2, 0, 1, s_split, False)
            mix(T, T - 1, 1, 1, s_split, False)

            pe.wait_ge(s_split, T)

            def gather(t, u, i, first):
                pe.wait_ge(tile_in[u], 16 * i + 16).then_inc(pe_passed, 1)
                if not first:
                    pe.wait_ge(o_step, t - 1).then_inc(pe_passed, 1)
                for j in range(T):
                    for q, s in enumerate((sh, sl)):
                        last = nc.tensor.matmul(po[u][:], tile[u][:, j, :].bitcast(fp8), s[:, j, :],
                                                start=(j == 0 and q == 0), stop=(j == T - 1 and q == 1))
                last.then_inc(gathered, 1)

            over_tiles(pe, gather)


def gat_gcn(nc, x, adj, w_seq, a1, a2, w_out, b_out, w1, b1, out):
    s1_rows = nc.dram_tensor("s1_rows", [H, N], fp32, kind="Internal").ap()
    g_rows = nc.dram_tensor("g_rows", [H, 1], fp32, kind="Internal").ap()
    x_t = x.rearrange("(t p) d -> t p d", p=P)
    adj_t = adj.rearrange("(t p) n -> t p n", p=P)
    out_t = out.rearrange("(t p) d -> t p d", p=P)
    with ExitStack() as ctx:
        adjT = ctx.enter_context(nc.sbuf_tensor("adjT", [P, T, T, P], u8))
        hid = ctx.enter_context(nc.sbuf_tensor("hid", [P, T, H, C], fp32))
        with ExitStack() as mid:
            AB = mid.enter_context(nc.sbuf_tensor("AB", [P, T, 2, H], fp32))
            S2 = mid.enter_context(nc.sbuf_tensor("S2", [P, H, 2, T], fp32))
            V = mid.enter_context(nc.sbuf_tensor("V", [P, H, T, CW], fp16))
            project_nodes(nc, x_t, adj_t, w_seq, a1, a2, s1_rows, g_rows, adjT, hid, V, AB, S2)
            attend(nc, s1_rows, adjT, V, AB, S2, hid)
        finish(nc, x_t, w_out, b_out, w1, b1, out_t, adjT, hid)


_INS = ['x', 'adj', 'L0_gnn_W_seq', 'L0_gnn_a1', 'L0_gnn_a2', 'L0_gnn_W_out', 'L0_gnn_b_out',
        'L1_gnn_weight', 'L1_gnn_bias']
_OUTS = [((2048, 512), 'float32')]


def kernel(**inputs):
    import numpy as _np
    import concourse.bacc as _bacc
    from concourse import mybir as _mybir
    from concourse.bass_utils import run_bass_kernel_spmd as _run

    nc = _bacc.Bacc("TRN2", target_bir_lowering=False, num_devices=1)
    arrays, args = {}, []
    for name in _INS:
        a = _np.ascontiguousarray(inputs[name])
        arrays[f"in_{name}_dram"] = a
        args.append(nc.dram_tensor(f"in_{name}_dram", a.shape, _mybir.dt.from_np(a.dtype), kind="ExternalInput").ap())
    for i, (shape, dtype) in enumerate(_OUTS):
        dt = _mybir.dt.from_np(_np.dtype(dtype))
        args.append(nc.dram_tensor(f"out_{i}_dram", shape, dt, kind="ExternalOutput").ap())
    gat_gcn(nc, *args)
    r = _run(nc, [arrays], core_ids=[0])
    return r.results[0]["out_0_dram"]
```

```python
import concourse.bass as bass
from concourse import mybir
from contextlib import ExitStack

P = 128
N = 2048
D = 512
H = 16
DH = D // H
T = N // P
KC = D // P
HALVES = 2
TH = T // HALVES
NH = N // HALVES
C = DH + 1
CV = 2 * C
CW = 2 * CV
PAIRS = H // 2
CH = 4
NCH = T // CH
BANK = 512
TB = BANK // CW
AG = [(0, 6), (6, 11), (11, 16)]
SLOPE = 0.2
STEEP = 2.0 ** 40
UP = 64.0
FP8_ONE = 56
EPS = 1e-5

fp32, fp16, bf16 = mybir.dt.float32, mybir.dt.float16, mybir.dt.bfloat16
fp8, u8, u32 = mybir.dt.float8e4, mybir.dt.uint8, mybir.dt.uint32
ALU = mybir.AluOpType
ACT = mybir.ActivationFunctionType
AX = mybir.AxisListType


def spread(ap, shape):
    return ap.to_broadcast(shape)


def project_nodes(nc, x, adj, w, a1, a2, s1_rows, adjT, hid, V, AB, S2):
    ctx = ExitStack()
    with ctx:
        def sb(name, shape, dt):
            return ctx.enter_context(nc.sbuf_tensor(name, shape, dt))

        def pb(name, shape, dt):
            return ctx.enter_context(nc.psum_tensor(name, shape, dt))

        def sem(name):
            return ctx.enter_context(nc.semaphore(name))

        WX = D + 2 * H
        at = sb("at", [P, 2, N], fp32)
        XB = N // D
        xt = at[:].rearrange("p u (q d) -> p (u q) d", q=XB)
        ab = sb("ab", [P, 2, N], fp16)
        parts = hid[:].rearrange("p t h c -> p (t h c)").bitcast(fp16)[:, 0:2 * T * D].rearrange(
            "p (w t k n) -> p w t k n", w=2, t=T, k=KC)
        xh, xl = parts[:, 0], parts[:, 1]
        wf = sb("wf", [P, KC, WX], fp32)
        wp = sb("wp", [P, 2, H, DH], fp32)
        wh = sb("wh", [P, KC, WX], fp16)
        wl = sb("wl", [P, KC, WX], fp16)
        av = sb("av", [P, 2, DH], fp32)
        sc = sb("sc", [P, T, 2, H], fp32)
        Vf = V[:].rearrange("p h t c -> p (h t c)")
        xr = Vf[:, 0:4 * N].rearrange("p (u w q d) -> p u w q d", u=2, w=2, q=XB)
        srow = Vf[0:2 * H, 4 * N:6 * N].bitcast(fp32)
        RB = BANK // P
        bmx = sb("bmx", [2 * H, T // RB], fp32)
        gmx = sb("gmx", [2 * H, 1], fp32)
        grow = sb("grow", [1, 2 * H], fp32)
        ones = sb("ones", [1, P], fp32)
        G = sb("G", [P, 2 * H], fp32)
        tt = sb("tt", [P, T, H], fp32)
        lr = sb("lr", [P, T, H], fp32)
        ea = sb("ea", [P, 2, T, H], fp32)
        F = sb("F", [P, 2, T, H], fp32)
        vt = wf[:].rearrange("p k n -> p (k n)")[:, 0:2 * H * CV].rearrange("p (u h a c) -> p u h a c", u=2, h=H, a=2)
        idf = sb("idf", [P, P], fp32)
        idb = sb("idb", [P, P], fp16)
        pxt = [pb(f"pxt{u}", [P, 2, KC, P], fp16) for u in range(2)]
        psq = [pb(f"psq{u}", [P, D], fp32) for u in range(2)]
        psc = [pb(f"psc{u}", [P, T * 2 * H], fp32) for u in range(2)]
        pat = [pb(f"pat{u}", [P, TH, P], fp16) for u in range(2)]
        rows = [psq[0][0:2 * H, :], psq[1][0:2 * H, :],
                *(p[0:2 * H].rearrange("h w a b -> h (w a b)").bitcast(fp32) for p in pxt)]

        w_loaded = sem("w_loaded")
        a_loaded = sem("a_loaded")
        x_loaded = [sem(f"x_loaded{u}") for u in range(2)]
        adj_loaded = [sem(f"adj_loaded{u}") for u in range(2)]
        ones_set = sem("ones_set")
        ident_ready = sem("ident_ready")
        w_prod = sem("w_prod")
        w_step = sem("w_step")
        w_high = sem("w_high")
        w_split = sem("w_split")
        wa_high = sem("wa_high")
        wa_split = sem("wa_split")
        x_turned = sem("x_turned")
        x_cast = sem("x_cast")
        x_split = sem("x_split")
        even_out = sem("even_out")
        odd_out = sem("odd_out")
        scored = sem("scored")
        row_out = sem("row_out")
        bank_max = sem("bank_max")
        nodes_turned = sem("nodes_turned")
        sc_ready = sem("sc_ready")
        row_max = sem("row_max")
        max_turned = sem("max_turned")
        max_row = sem("max_row")
        max_spread = sem("max_spread")
        g_ready = sem("g_ready")
        row_stored = sem("row_stored")
        e_step = sem("e_step")
        exp_in = sem("exp_in")
        exp_out = sem("exp_out")
        edges_cast = sem("edges_cast")
        adj_turned = sem("adj_turned")
        adj_out = sem("adj_out")
        projected = sem("projected")
        scaled = sem("scaled")
        v_high = sem("v_high")
        v_split = sem("v_split")
        pool_passed = sem("pool_passed_a")

        BODY = 2 * XB
        block = ctx.enter_context(nc.Block())

        @block.sync
        def _(sp):
            sp.dma_start(av[:, 0, :], a1[None, :].to_broadcast([P, DH])).then_inc(a_loaded, 16)
            sp.dma_start(av[:, 1, :], a2[None, :].to_broadcast([P, DH])).then_inc(a_loaded, 16)
            for b in range(T // XB):
                u = b % 2
                if b == 1:
                    sp.dma_start(wf[:, :, 0:D], w.rearrange("(k p) n -> p k n", p=P)).then_inc(w_loaded, 16)
                if b >= 2:
                    sp.wait_ge(x_split, b - 1)
                sp.dma_start(xt[:, u * XB:(u + 1) * XB, :],
                             x[b * XB:(b + 1) * XB, :, :].rearrange("q p d -> p q d")).then_inc(x_loaded[u], 16)

            def load(t, u, first):
                if first:
                    sp.wait_ge(x_split, T // XB - 1 + u)
                else:
                    sp.wait_ge(edges_cast, t - 1)
                sp.dma_start(at[:, u, :], adj[t, :, :]).then_inc(adj_loaded[u], 16)

            for u in range(2):
                load(u, u, True)
            with sp.Fori(1, T // 2) as i:
                for u in range(2):
                    load(2 * i + u, u, False)
            sp.wait_ge(row_stored, 16)

        @block.gpsimd
        def _(pool):
            nc.gpsimd.memset(idf[:], 1.0).then_inc(ones_set, 1)
            nc.gpsimd.memset(idb[:], 1.0).then_inc(ones_set, 1)
            nc.gpsimd.memset(ones[:], 1.0).then_inc(ones_set, 1)
            pool.wait_ge(ones_set, 3)
            for m in (idf, idb):
                nc.gpsimd.affine_select(out=m[:], in_=m[:], compare_op=ALU.is_equal, fill=0.0, base=0,
                                        pattern=[[-1, P]], channel_multiplier=1).then_inc(ident_ready, 1)
            pool.wait_ge(w_loaded, 16)
            pool.wait_ge(a_loaded, 32)
            for k in range(KC):
                for s in range(2):
                    if k:
                        pool.wait_ge(w_step, 2 * k + s - 1)
                    nc.gpsimd.tensor_tensor(wp[:, s], wf[:, k, 0:D].rearrange("p (h d) -> p h d", h=H),
                                            spread(av[:, s:s + 1, :], [P, H, DH]), ALU.mult).then_inc(w_prod, 1)

            def low(t, u):
                pool.wait_ge(v_high, t + 1).then_inc(pool_passed, 1)
                nc.gpsimd.tensor_tensor(V[:, :, t, CV:CW], vt[:, u].rearrange("p h a c -> p h (a c)"),
                                        V[:, :, t, 0:CV], ALU.subtract).then_inc(v_split, 1)

            with pool.Fori(0, T // 2) as i:
                for u in range(2):
                    low(2 * i + u, u)

        @block.scalar
        def _(act):
            def cut(b):
                act.wait_ge(x_loaded[b % 2], 16 * (b // 2 + 1))
                if b >= 2:
                    act.wait_ge(x_turned, XB * (b - 1))
                nc.scalar.activation(xr[:, b % 2, 0], xt[:, b % 2 * XB:(b % 2 + 1) * XB, :],
                                     ACT.Copy).then_inc(x_cast, 1)

            cut(0)
            cut(1)
            for t in range(0, T, 2):
                act.wait_ge(x_turned, t + 1)
                nc.scalar.activation(parts[:, :, t].rearrange("p w k n -> p w (k n)"),
                                     pxt[0][:].rearrange("p w k n -> p w (k n)"), ACT.Copy).then_inc(even_out, 1)
                if t % XB == XB - 2 and t // XB + 2 < T // XB:
                    cut(t // XB + 2)
            act.wait_ge(w_step, 2 * KC)
            nc.scalar.activation(wh[:, :, D:WX], wf[:, :, D:WX], ACT.Copy, scale=UP).then_inc(wa_high, 1)
            nc.scalar.activation(wh[:, :, 0:D], wf[:, :, 0:D], ACT.Copy, scale=UP).then_inc(w_high, 1)
            for b in range(T // RB):
                act.wait_ge(scored, b + 1)
                nc.scalar.activation(srow[:, b * BANK:(b + 1) * BANK], rows[b], ACT.Copy,
                                     scale=1.0 / UP).then_inc(row_out, 1)
            act.wait_ge(row_out, 4)
            act.dma_start(s1_rows[:, :], srow[0:H, :]).then_inc(row_stored, 16)
            act.wait_ge(exp_in, 1)
            nc.scalar.activation(F[:, 0], tt[:], ACT.Exp).then_inc(exp_out, 1)
            nc.scalar.activation(F[:, 1], tt[:], ACT.Exp, scale=SLOPE).then_inc(exp_out, 1)
            act.wait_ge(e_step, 4)
            nc.scalar.activation(ea[:], ea[:], ACT.Exp).then_inc(exp_out, 1)
            act.wait_ge(row_stored, 16)

            def edges_out(t):
                for f in range(2):
                    act.wait_ge(adj_turned, 2 * t + f + 1)
                    nc.scalar.activation(adjT[:, t, f * TH:(f + 1) * TH, :], pat[f][:], ACT.Copy,
                                         scale=float(FP8_ONE)).then_inc(adj_out, 1)

            def high(t, u):
                act.wait_ge(scaled, 2 * t + 2)
                nc.scalar.activation(V[:, :, t, 0:CV], vt[:, u].rearrange("p h a c -> p h (a c)"),
                                     ACT.Copy).then_inc(v_high, 1)

            edges_out(0)
            with act.Fori(0, T // 2 - 1) as i:
                for u in range(2):
                    edges_out(2 * i + u + 1)
                    high(2 * i + u, u)
            edges_out(T - 1)
            high(T - 2, 0)
            high(T - 1, 1)

        @block.vector
        def _(dve):
            for n, free in enumerate((even_out, odd_out)):
                nc.vector.memset(G[:, n:n + 1], 0.0).then_inc(free, 1)

            def cut(b):
                dve.wait_ge(x_cast, b + 1)
                if b >= 2:
                    dve.wait_ge(x_turned, XB * (b - 1))
                nc.vector.tensor_tensor(xr[:, b % 2, 1], xt[:, b % 2 * XB:(b % 2 + 1) * XB, :], xr[:, b % 2, 0],
                                        ALU.subtract).then_inc(x_split, 1)

            cut(0)
            cut(1)
            for t in range(1, T, 2):
                dve.wait_ge(x_turned, t + 1)
                nc.vector.tensor_copy(parts[:, :, t], pxt[1][:]).then_inc(odd_out, 1)
                if t % XB == XB - 1 and t // XB + 2 < T // XB:
                    cut(t // XB + 2)
                k, s = divmod(t // 2, 2)
                dve.wait_ge(w_prod, 2 * k + s + 1)
                nc.vector.tensor_reduce(wf[:, k, D + s * H:D + (s + 1) * H], wp[:, s], AX.X,
                                        ALU.add).then_inc(w_step, 1)

            def split(c0, c1, high, done):
                dve.wait_ge(high, 1)
                nc.vector.scalar_tensor_tensor(wl[:, :, c0:c1], wf[:, :, c0:c1], UP, wh[:, :, c0:c1],
                                               ALU.mult, ALU.subtract).then_inc(done, 1)

            def cast(t, u, i, first):
                dve.wait_ge(adj_loaded[u], 16 * i + 16)
                if not first:
                    dve.wait_ge(adj_turned, 2 * t - 2)
                nc.vector.tensor_copy(ab[:, u], at[:, u]).then_inc(edges_cast, 1)

            split(D, WX, wa_high, wa_split)
            split(0, D, w_high, w_split)
            for b in range(T // RB):
                dve.wait_ge(row_out, b + 1)
                nc.vector.tensor_reduce(bmx[:, b:b + 1], srow[:, b * BANK:(b + 1) * BANK], AX.X,
                                        ALU.max).then_inc(bank_max, 1)
            dve.wait_ge(bank_max, T // RB)
            nc.vector.tensor_reduce(gmx[:], bmx[:], AX.X, ALU.max).then_inc(row_max, 1)
            cast(0, 0, 0, True)
            dve.wait_ge(max_turned, 1)
            nc.vector.tensor_copy(grow[:], psc[1][0:1, 0:2 * H]).then_inc(max_row, 1)
            dve.wait_ge(nodes_turned, 1)
            nc.vector.tensor_copy(sc[:].rearrange("p t s h -> p (t s h)"), psc[0][:]).then_inc(sc_ready, 1)
            dve.wait_ge(sc_ready, 1)
            nc.vector.tensor_scalar(S2[:, :, 0, :], sc[:, :, 1, :].rearrange("p t h -> p h t"), -1.0, None, ALU.mult)
            nc.vector.tensor_scalar(S2[:, :, 1, :], sc[:, :, 1, :].rearrange("p t h -> p h t"), STEEP, None, ALU.mult)
            dve.wait_ge(max_spread, 1)
            nc.vector.tensor_copy(G[:], psc[1][:, 0:2 * H]).then_inc(g_ready, 1)
            dve.wait_ge(g_ready, 1)
            g = spread(G[:, None, H:2 * H], [P, T, H])
            nc.vector.tensor_tensor(tt[:], sc[:, :, 1, :], g, ALU.subtract).then_inc(exp_in, 1)
            dve.wait_ge(exp_out, 2)
            nc.vector.tensor_tensor(tt[:], sc[:, :, 0, :], g, ALU.add).then_inc(e_step, 1)
            dve.wait_ge(e_step, 1)
            nc.vector.scalar_tensor_tensor(lr[:], tt[:], SLOPE, tt[:], ALU.mult, ALU.max).then_inc(e_step, 1)
            dve.wait_ge(e_step, 2)
            nc.vector.tensor_tensor(ea[:, 0], tt[:], lr[:], ALU.subtract).then_inc(e_step, 1)
            nc.vector.scalar_tensor_tensor(ea[:, 1], tt[:], SLOPE, lr[:], ALU.mult, ALU.subtract).then_inc(e_step, 1)
            def weigh(t, u, first):
                dve.wait_ge(projected, t + 1)
                if not first:
                    dve.wait_ge(v_split, t - 1)
                nc.vector.tensor_tensor(vt[:, u, :, :, 0:DH],
                                        spread(psq[u][:].rearrange("p (h d) -> p h d", h=H)[:, :, None, :],
                                               [P, H, 2, DH]),
                                        spread(F[:, :, t, :].rearrange("p a h -> p h a")[:, :, :, None],
                                               [P, H, 2, DH]), ALU.mult).then_inc(scaled, 1)
                nc.vector.tensor_scalar(vt[:, u, :, :, DH], F[:, :, t, :].rearrange("p a h -> p h a"), UP, None,
                                        ALU.mult).then_inc(scaled, 1)

            cast(1, 1, 0, True)
            weigh(0, 0, True)
            dve.wait_ge(exp_out, 3)
            nc.vector.tensor_copy(AB[:, :, 0, :], ea[:, 0])
            nc.vector.tensor_scalar(AB[:, :, 1, :], ea[:, 1], -1.0, None, ALU.mult)
            cast(2, 0, 1, False)
            cast(3, 1, 1, False)
            weigh(1, 1, True)
            with dve.Fori(1, T // 2 - 1) as i:
                for u in range(2):
                    cast(2 * i + 2 + u, u, i + 1, False)
                    weigh(2 * i + u, u, False)
            weigh(T - 2, 0, False)
            weigh(T - 1, 1, False)

        @block.tensor
        def _(pe):
            PARTS = ((xh, wh), (xh, wl), (xl, wh))
            pe.wait_ge(ident_ready, 2)
            with pe.Fori(0, T // BODY) as i:
                for v in range(BODY):
                    t = BODY * i + v
                    if v % XB == 0:
                        pe.wait_ge(x_split, 2 * i + v // XB + 1)
                    pe.wait_ge((even_out, odd_out)[v % 2], XB * i + v // 2 + 1)
                    for w in range(2):
                        for k in range(KC):
                            last = nc.tensor.transpose(pxt[v % 2][:, w, k, :],
                                                       xr[:, v // XB, w, v % XB, k * P:(k + 1) * P], idb[:])
                    last.then_inc(x_turned, 1)
            pe.wait_ge(even_out, 1 + T // 2)
            pe.wait_ge(odd_out, 1 + T // 2)
            pe.wait_ge(wa_split, 1)
            for b in range(T // RB):
                for k in range(KC):
                    for m, (lhs, rhs) in enumerate(PARTS):
                        last = nc.tensor.matmul(rows[b], rhs[:, k, D:WX], lhs[:, b * RB:(b + 1) * RB, k, :],
                                                start=(k == 0 and m == 0), stop=(k == KC - 1 and m == 2))
                last.then_inc(scored, 1)

            def project(t, u, first):
                if not first:
                    pe.wait_ge(scaled, 2 * t - 2)
                for k in range(KC):
                    for m, (lhs, rhs) in enumerate(PARTS):
                        last = nc.tensor.matmul(psq[u][:], lhs[:, t, k, :], rhs[:, k, 0:D],
                                                start=(k == 0 and m == 0), stop=(k == KC - 1 and m == 2))
                last.then_inc(projected, 1)

            def turn_edges(t, u, very_first):
                pe.wait_ge(edges_cast, t + 1)
                for f in range(2):
                    if not very_first:
                        pe.wait_ge(adj_out, 2 * t + f - 1)
                    for b in range(TH):
                        c = (f * TH + b) * P
                        last = nc.tensor.transpose(pat[f][:, b, :], ab[:, u, c:c + P], idb[:])
                    last.then_inc(adj_turned, 1)

            pe.wait_ge(row_out, T // RB)
            for t in range(T):
                last = nc.tensor.transpose(psc[0][:, t * 2 * H:(t + 1) * 2 * H], srow[:, t * P:(t + 1) * P],
                                           idf[0:2 * H, 0:2 * H])
            last.then_inc(nodes_turned, 1)
            pe.wait_ge(row_max, 1)
            nc.tensor.transpose(psc[1][0:1, 0:2 * H], gmx[:], idf[0:2 * H, 0:2 * H]).then_inc(max_turned, 1)
            turn_edges(0, 0, True)
            pe.wait_ge(max_row, 1)
            nc.tensor.matmul(psc[1][:, 0:2 * H], ones[:], grow[:], start=True, stop=True).then_inc(max_spread, 1)
            pe.wait_ge(w_split, 1)
            project(0, 0, True)
            turn_edges(1, 1, False)
            project(1, 1, True)
            turn_edges(2, 0, False)
            with pe.Fori(1, T // 2 - 1) as i:
                turn_edges(2 * i + 1, 1, False)
                project(2 * i, 0, False)
                turn_edges(2 * i + 2, 0, False)
                project(2 * i + 1, 1, False)
            turn_edges(T - 1, 1, False)
            project(T - 2, 0, False)
            project(T - 1, 1, False)


def attend(nc, s1_rows, adjT, V, AB, S2, hid):
    ctx = ExitStack()
    with ctx:
        def sb(name, shape, dt):
            return ctx.enter_context(nc.sbuf_tensor(name, shape, dt))

        def pb(name, shape, dt):
            return ctx.enter_context(nc.psum_tensor(name, shape, dt))

        def sem(name):
            return ctx.enter_context(nc.semaphore(name))

        edge = [sb(f"edge{a}", [P, T, NH], u8) for a in range(2)]
        vcur = [sb(f"vcur{a}", [P, T, CW], fp16) for a in range(2)]
        s1b = [sb(f"s1b{a}", [P, NH], fp32) for a in range(2)]
        s2c = [sb(f"s2c{a}", [P, 2, T], fp32) for a in range(2)]
        tile = sb("tile", [P, T, P], u8)
        esum = [sb(f"esum{a}", [P, TH, CW], fp32) for a in range(2)]
        asum = sb("asum", [P, H, CV], fp32)
        pair = sb("pair", [P, TH, 2, C], fp32)
        plain = sb("plain", [P, H, C], fp32)
        pe_e = [pb(f"pe_e{a}", [P, 3, BANK], fp32) for a in range(2)]
        pe_a = [pb(f"pe_a{b}", [P, BANK], fp32) for b in range(2)]

        head_in = [sem(f"head_in{a}") for a in range(2)]
        v_in = [sem(f"v_in{a}") for a in range(2)]
        tile_in = sem("tile_in")
        act_passed = sem("act_passed")
        pe_passed = sem("pe_passed")
        pool_passed = sem("pool_passed")
        act_sign = sem("act_sign")
        dve_sign = sem("dve_sign")
        masked = sem("masked")
        head_done = sem("head_done")
        plain_done = sem("plain_done")
        head_out = sem("head_out")
        plain_out = sem("plain_out")
        joined = sem("joined")
        joined_a = sem("joined_a")
        p_step = sem("p_step")
        q_step = sem("q_step")

        ITER = HALVES * PAIRS
        assert ITER == T
        block = ctx.enter_context(nc.Block())

        @block.sync
        def _(sp):
            def load(it, half, p, first):
                for a in range(2):
                    g = 2 * it + a
                    if not first:
                        sp.wait_ge(masked, NCH * (g - 1))
                    sp.dma_start(s1b[a][:], s1_rows[bass.ds(2 * p + a, 1), bass.ds(half * NH, NH)]
                                 .to_broadcast([P, NH])).then_inc(head_in[a], 16)
                    sp.dma_start(s2c[a][:], S2[:, 2 * p + a, :, :]).then_inc(head_in[a], 16)
                    if not first:
                        sp.wait_ge(head_done, g - 1)
                    sp.dma_start(vcur[a][:], V[:, 2 * p + a, :, :]).then_inc(v_in[a], 16)
                    if a == 0:
                        if not first:
                            sp.wait_ge(plain_done, 3 * it)
                        sp.dma_start(tile[:], adjT[:, it, :, :]).then_inc(tile_in, 16)

            load(0, 0, 0, True)
            with sp.Fori(1, PAIRS) as p:
                load(p, 0, p, False)
            with sp.Fori(0, PAIRS) as p:
                load(p + PAIRS, 1, p, False)

        @block.scalar
        def _(act):
            def evict(g, a, first):
                act.wait_ge(head_done, g + 1)
                if not first:
                    act.wait_ge(joined, g)
                nc.scalar.activation(esum[a][:, 0:2 * TB, :].rearrange("p (b t) c -> p b (t c)", b=2),
                                     pe_e[a][:, 0:2, 0:TB * CW], ACT.Copy).then_inc(head_out, 1)
                nc.scalar.activation(esum[a][:, 2 * TB:TH, :].rearrange("p t c -> p (t c)"),
                                     pe_e[a][:, 2, 0:(TH - 2 * TB) * CW], ACT.Copy).then_inc(head_out, 1)

            def slots(it, first):
                for a in range(2):
                    g = 2 * it + a
                    act.wait_ge(head_in[a], 32 * it + 32)
                    if not first:
                        act.wait_ge(head_done, g - 1).then_inc(act_passed, 1)
                    for c in range(NCH):
                        for j in range(CH * c + CH // 2, CH * (c + 1)):
                            ins = nc.scalar.activation(edge[a][:, j, :].bitcast(fp8), s1b[a][:], ACT.Sigmoid,
                                                       bias=s2c[a][:, 1, j:j + 1], scale=STEEP, saturate=False)
                        ins.then_inc(act_sign, 1)
                    if not (first and a == 0):
                        evict(g - 1, 1 - a, first)

            slots(0, True)
            with act.Fori(1, ITER) as it:
                slots(it, False)
            evict(2 * ITER - 1, 1, False)

        @block.vector
        def _(dve):
            def evict_plain(n, k):
                h0, h1 = AG[k]
                dve.wait_ge(plain_done, n + 1)
                nc.vector.tensor_copy(asum[:, h0:h1, :].rearrange("p h c -> p (h c)"),
                                      pe_a[k % 2][:, 0:(h1 - h0) * CV]).then_inc(plain_out, 1)

            def slots(it, half, first):
                for a in range(2):
                    g = 2 * it + a
                    dve.wait_ge(head_in[a], 32 * it + 32)
                    if not first:
                        dve.wait_ge(head_done, g - 1)

                    def sign(c):
                        for j in range(CH * c, CH * c + CH // 2):
                            ins = nc.vector.tensor_scalar(edge[a][:, j, :], s1b[a][:], s2c[a][:, 0, j:j + 1],
                                                          float(FP8_ONE), ALU.is_gt, ALU.mult)
                        ins.then_inc(dve_sign, 1)

                    sign(0)
                    for c in range(NCH):
                        if c + 1 < NCH:
                            sign(c + 1)
                        dve.wait_ge(act_sign, NCH * g + c + 1)
                        dve.wait_ge(dve_sign, NCH * g + c + 1)
                        e = edge[a][:, CH * c:CH * (c + 1), :].rearrange("p j (t i) -> p j t i", t=TH).bitcast(u32)
                        m = adjT[:, half * TH:(half + 1) * TH, CH * c:CH * (c + 1), :].rearrange(
                            "p t j i -> p j t i").bitcast(u32)
                        nc.vector.tensor_tensor(e, e, m, ALU.bitwise_and).then_inc(masked, 1)
                    if a == 1:
                        if not first:
                            dve.wait_ge(joined_a, it)
                        evict_plain(3 * it, 0)
                    elif not first:
                        evict_plain(3 * it - 2, 1)
                        evict_plain(3 * it - 1, 2)

            slots(0, 0, True)
            with dve.Fori(1, PAIRS) as p:
                slots(p, 0, False)
            with dve.Fori(0, PAIRS) as p:
                slots(p + PAIRS, 1, False)
            evict_plain(3 * ITER - 2, 1)
            evict_plain(3 * ITER - 1, 2)

        @block.tensor
        def _(pe):
            def plain_sum(it, k, first):
                h0, h1 = AG[k]
                if k == 2 or not first:
                    pe.wait_ge(plain_out, 3 * it + (0, -1, 1)[k]).then_inc(pe_passed, 1)
                if k == 0:
                    pe.wait_ge(tile_in, 16 * it + 16).then_inc(pe_passed, 1)
                for j in range(T):
                    ins = nc.tensor.matmul(pe_a[k % 2][:, 0:(h1 - h0) * CV], tile[:, j, :].bitcast(fp8),
                                           V[:, h0:h1, j, :].rearrange("p h (w c) -> p h w c", w=2)[:, :, :, C:CV],
                                           start=(j == 0), stop=(j == T - 1))
                ins.then_inc(plain_done, 1)

            def slots(it, first):
                for a in range(2):
                    g = 2 * it + a
                    for k in ((0,), (1, 2))[a]:
                        plain_sum(it, k, first)
                    pe.wait_ge(v_in[a], 16 * it + 16)
                    if not first:
                        pe.wait_ge(head_out, 2 * g - 2)
                    for c in range(NCH):
                        pe.wait_ge(masked, NCH * g + c + 1).then_inc(pe_passed, 1)
                        for j in range(CH * c, CH * (c + 1)):
                            for i in range(TH):
                                b, o = i // TB, (i % TB) * CW
                                ins = nc.tensor.matmul(pe_e[a][:, b, o:o + CW],
                                                       edge[a][:, j, i * P:(i + 1) * P].bitcast(fp8), vcur[a][:, j, :],
                                                       start=(j == 0 and i % TB == 0), stop=(j == T - 1),
                                                       skip_group_check=True)
                    ins.then_inc(head_done, 1)

            slots(0, True)
            with pe.Fori(1, ITER) as it:
                slots(it, False)

        @block.gpsimd
        def _(pool):
            nc.gpsimd.memset(hid[:], 0.0).then_inc(joined, 1)
            pool.wait_ge(joined, 1)

            def join(g, half, h, a):
                pool.wait_ge(head_out, 2 * g + 2)
                nc.gpsimd.tensor_tensor(pair[:].rearrange("p t s c -> p t (s c)"), esum[a][:, :, 0:CV],
                                        esum[a][:, :, CV:CW], ALU.add).then_inc(joined, 1)
                pool.wait_ge(joined, g + 2).then_inc(pool_passed, 1)
                nc.gpsimd.tensor_tensor(pair[:], pair[:],
                                        spread(AB[:, half * TH:(half + 1) * TH, :, bass.ds(h, 1)],
                                               [P, TH, 2, C]), ALU.mult).then_inc(p_step, 1)
                for s in range(2):
                    pool.wait_ge(p_step, 3 * g + s + 1).then_inc(pool_passed, 1)
                    nc.gpsimd.tensor_tensor(hid[:, half * TH:(half + 1) * TH, h, :],
                                            hid[:, half * TH:(half + 1) * TH, h, :], pair[:, :, s, :],
                                            ALU.add).then_inc(p_step, 1)
                pool.wait_ge(p_step, 3 * g + 3)

            def join_plain(t):
                pool.wait_ge(plain_out, 3 * t + 3)
                nc.gpsimd.tensor_tensor(plain[:], asum[:, :, 0:C], asum[:, :, C:CV], ALU.add).then_inc(joined_a, 1)
                pool.wait_ge(joined_a, t + 1).then_inc(pool_passed, 1)
                nc.gpsimd.tensor_tensor(plain[:], plain[:], spread(AB[:, t, 1, :][:, :, None], [P, H, C]),
                                        ALU.mult).then_inc(q_step, 1)
                pool.wait_ge(q_step, 2 * t + 1).then_inc(pool_passed, 1)
                nc.gpsimd.tensor_tensor(hid[:, t], hid[:, t], plain[:], ALU.subtract).then_inc(q_step, 1)
                pool.wait_ge(q_step, 2 * t + 2)

            join(0, 0, 0, 0)
            with pool.Fori(1, PAIRS) as p:
                join(2 * p - 1, 0, 2 * p - 1, 1)
                join_plain(p - 1)
                join(2 * p, 0, 2 * p, 0)
            join(H - 1, 0, H - 1, 1)
            join_plain(PAIRS - 1)
            join(H, 1, 0, 0)
            with pool.Fori(1, PAIRS) as p:
                join(H + 2 * p - 1, 1, 2 * p - 1, 1)
                join_plain(PAIRS + p - 1)
                join(H + 2 * p, 1, 2 * p, 0)
            join(2 * H - 1, 1, H - 1, 1)
            join_plain(T - 1)


def finish(nc, x, w_out, b_out, w1, b1, out, adjT, hid):
    ctx = ExitStack()
    with ctx:
        def sb(name, shape, dt):
            return ctx.enter_context(nc.sbuf_tensor(name, shape, dt))

        def pb(name, shape, dt):
            return ctx.enter_context(nc.psum_tensor(name, shape, dt))

        def sem(name):
            return ctx.enter_context(nc.semaphore(name))

        wf = [sb(f"wf{m}", [P, KC, D], fp32) for m in range(2)]
        wh = [sb(f"wh_{m}", [P, KC, D], fp16) for m in range(2)]
        wl = [sb(f"wl_{m}", [P, KC, D], fp16) for m in range(2)]
        bias = sb("bias", [P, 2, D], fp32)
        idb = sb("idb2", [P, P], fp16)
        xr = sb("xr", [P, 2, D], fp32)
        rec = sb("rec", [P, T, H], fp32)
        ht = sb("ht", [P, 2, D], fp32)
        hp = sb("hp", [P, 2, 2, D], fp16)
        h_t = sb("h_t", [P, 2, 2, KC, P], fp16)
        y = sb("y", [P, 2, D], fp32)
        ye = sb("ye", [P, 2, D], fp32)
        z = sb("z", [P, 2, D], fp32)
        st = sb("st", [P, 2, 6], fp32)
        mv = sb("mv", [P, 2, 2], fp32)
        ve = sb("ve", [P, 2, 1], fp32)
        rs = sb("rs", [P, 2, 1], fp32)
        consts = sb("consts", [P, 2], fp32)
        x1 = hid[:].rearrange("p t h c -> p t (h c)")[:, :, 0:D]
        xp = sb("xp", [P, 2, 2, D], fp16)
        x_t = sb("x_t", [P, 2, 2, KC, P], fp16)
        sh = sb("sh", [P, T, D], fp16)
        sl = sb("sl", [P, T, D], fp16)
        tile = [sb(f"tile_{u}", [P, T, P], u8) for u in range(2)]
        ph = [pb(f"ph{u}", [P, 2, KC, P], fp16) for u in range(2)]
        px = [pb(f"px{u}", [P, 2, KC, P], fp16) for u in range(2)]
        pm = [pb(f"pm{u}", [P, D], fp32) for u in range(2)]
        ps = [pb(f"ps{u}", [P, D], fp32) for u in range(2)]
        po = [p[:].rearrange("p w k n -> p (w k n)").bitcast(fp32) for p in ph]

        w_in = [sem(f"w_in{m}") for m in range(2)]
        b_in = sem("b_in")
        ones_set = sem("ones_set2")
        ident_ready = sem("ident2")
        w_high = sem("w_high2")
        w_split = sem("w_split2")
        x_in = [sem(f"x_in{u}") for u in range(2)]
        tile_in = [sem(f"tile_in{u}") for u in range(2)]
        rec_ready = sem("rec_ready")
        h_ready = sem("h_ready")
        h_high = sem("h_high")
        h_split = sem("h_split")
        h_turned = sem("h_turned")
        h_out = sem("h_out")
        mixed = sem("mixed")
        y_ready = sem("y_ready")
        y_neg = sem("y_neg")
        y_exp = sem("y_exp")
        y_pos = sem("y_pos")
        y_elu = sem("y_elu")
        z_ready = sem("z_ready")
        stats_ready = sem("stats_ready")
        var_ready = sem("var_ready")
        eps_added = sem("eps_added")
        rstd_ready = sem("rstd_ready")
        x1_ready = sem("x1_ready")
        x_high = sem("x_high")
        x_split = sem("x_split2")
        x_turned = sem("x_turned2")
        x_out = sem("x_out")
        supported = sem("supported")
        s_high = sem("s_high")
        s_split = sem("s_split")
        gathered = sem("gathered")
        xb_ready = sem("xb_ready")
        o_sum = sem("o_sum")
        o_ready = sem("o_ready")
        stored = [sem(f"stored{u}") for u in range(2)]
        dve_passed = sem("dve_passed")
        pe_passed = sem("pe_passed2")

        def exists(t):
            return not isinstance(t, int) or 0 <= t < T

        def later(t):
            return not isinstance(t, int) or t >= 2

        def slots(eng, slot, first, last):
            lo, hi = 4, T - 4
            for k in range(first, lo):
                slot(k, k % 2)
            with eng.Fori(lo // 2, hi // 2) as i:
                for u in range(2):
                    slot(2 * i + u, u)
            for k in range(hi, last + 1):
                slot(k, k % 2)

        def over_tiles(eng, slot):
            for u in range(2):
                slot(u, u, 0, True)
            with eng.Fori(1, T // 2) as i:
                for u in range(2):
                    slot(2 * i + u, u, i, False)

        block = ctx.enter_context(nc.Block())

        @block.sync
        def _(sp):
            for k in range(KC):
                sp.dma_start(wf[0][:, k], w_out[k * P:(k + 1) * P, :]).then_inc(w_in[0], 16)
            sp.dma_start(wf[1][:], w1.rearrange("(k p) n -> p k n", p=P)).then_inc(w_in[1], 16)

            def load(t, u, i, first):
                if not first:
                    sp.wait_ge(z_ready, t - 1)
                sp.dma_start(xr[:, u, :], x[t, :, :]).then_inc(x_in[u], 16)

            over_tiles(sp, load)

            def edges(t, u, i, first):
                if not first:
                    sp.wait_ge(gathered, t - 1)
                sp.dma_start(tile[u][:], adjT[:, t, :, :]).then_inc(tile_in[u], 16)

            over_tiles(sp, edges)

        @block.gpsimd
        def _(pool):
            nc.gpsimd.memset(idb[:], 1.0).then_inc(ones_set, 1)
            nc.gpsimd.memset(consts[:, 0:1], EPS).then_inc(ones_set, 1)
            nc.gpsimd.memset(consts[:, 1:2], -0.5).then_inc(ones_set, 1)
            pool.wait_ge(ones_set, 3)
            nc.gpsimd.affine_select(out=idb[:], in_=idb[:], compare_op=ALU.is_equal, fill=0.0, base=0,
                                    pattern=[[-1, P]], channel_multiplier=1).then_inc(ident_ready, 1)
            pool.wait_ge(rec_ready, 1)

            def rstd(n, t, u):
                pool.wait_ge(var_ready, n + t + 1)
                nc.gpsimd.tensor_tensor(ve[:, u], mv[:, u, 1:2], consts[:, 0:1], ALU.add).then_inc(eps_added, 1)
                pool.wait_ge(eps_added, n + t + 1)
                nc.gpsimd.tensor_tensor(rs[:, u], ve[:, u], consts[:, 1:2], ALU.pow).then_inc(rstd_ready, 1)

            def normalise(t, u):
                if later(t):
                    pool.wait_ge(h_split, t - 1)
                nc.gpsimd.tensor_tensor(ht[:, u, :].rearrange("p (h d) -> p h d", h=H), hid[:, t, :, 0:DH],
                                        spread(rec[:, t, :][:, :, None], [P, H, DH]), ALU.mult).then_inc(h_ready, 1)

            def residual(t, u, i):
                pool.wait_ge(x_in[u], 16 * i + 16)
                if later(t):
                    pool.wait_ge(x1_ready, t - 1)
                pool.wait_ge(y_elu, t + 1)
                nc.gpsimd.tensor_tensor(z[:, u], ye[:, u], xr[:, u], ALU.add).then_inc(z_ready, 1)

            def slot(k, u, i):
                if exists(k):
                    residual(k, u, i)
                    rstd(0, k, u)
                if exists(k + 4):
                    normalise(k + 4, u)

            for k in range(-4, 2):
                slot(k, k % 2, k // 2)
            with pool.Fori(1, T // 2 - 2) as i:
                for u in range(2):
                    slot(2 * i + u, u, i)
            for k in range(T - 4, T):
                slot(k, k % 2, k // 2)

            def with_bias(t, u, i, first):
                if not first:
                    pool.wait_ge(o_sum, t - 1)
                nc.gpsimd.tensor_tensor(ye[:, u], x1[:, t, :], bias[:, 1, :], ALU.add).then_inc(xb_ready, 1)

            pool.wait_ge(x1_ready, T)
            pool.wait_ge(b_in, 32)
            with_bias(0, 0, 0, True)
            with_bias(1, 1, 0, True)
            rstd(T, 0, 0)
            with_bias(2, 0, 1, False)
            rstd(T, 1, 1)
            with pool.Fori(1, T // 2 - 1) as i:
                for u in range(2):
                    with_bias(2 * i + u + 1, 1 - u, i, False)
                    rstd(T, 2 * i + u, u)
            with_bias(T - 1, 1, 0, False)
            rstd(T, T - 2, 0)
            rstd(T, T - 1, 1)

        @block.scalar
        def _(act):
            for m, src in enumerate((b_out, b1)):
                act.dma_start(bias[:, m, :], src[None, :].to_broadcast([P, D])).then_inc(b_in, 16)

            def h_cast(t, u):
                act.wait_ge(h_ready, t + 1)
                if later(t):
                    act.wait_ge(h_turned, t - 1)
                nc.scalar.activation(hp[:, u, 0], ht[:, u], ACT.Copy).then_inc(h_high, 1)

            def h_evict(t, u):
                act.wait_ge(h_turned, t + 1)
                if later(t):
                    act.wait_ge(mixed, t - 1)
                nc.scalar.activation(h_t[:, u].rearrange("p w k n -> p (w k n)"),
                                     ph[u][:].rearrange("p w k n -> p (w k n)"), ACT.Copy).then_inc(h_out, 1)

            def elu(t, u):
                act.wait_ge(y_ready, t + 1)
                if later(t):
                    act.wait_ge(z_ready, t - 1)
                nc.scalar.activation(ye[:, u], y[:, u], ACT.Relu, scale=-1.0).then_inc(y_neg, 1)
                act.wait_ge(y_neg, t + 1)
                nc.scalar.activation(ye[:, u], ye[:, u], ACT.Exp, scale=-1.0).then_inc(y_exp, 1)

            def x_cast(t, u):
                act.wait_ge(x1_ready, t + 1)
                if later(t):
                    act.wait_ge(x_turned, t - 1)
                nc.scalar.activation(xp[:, u, 0], x1[:, t, :], ACT.Copy).then_inc(x_high, 1)

            def x_evict(t, u):
                act.wait_ge(x_turned, t + 1)
                if later(t):
                    act.wait_ge(supported, t - 1)
                nc.scalar.activation(x_t[:, u].rearrange("p w k n -> p (w k n)"),
                                     px[u][:].rearrange("p w k n -> p (w k n)"), ACT.Copy).then_inc(x_out, 1)

            def s_out(t, u):
                act.wait_ge(supported, t + 1)
                nc.scalar.activation(sh[:, t, :], ps[u][:], ACT.Copy).then_inc(s_high, 1)

            def slot(k, u):
                for stage, t in ((x_cast, k - 1), (elu, k), (h_evict, k + 2), (s_out, k - 2), (x_evict, k - 1),
                                 (h_cast, k + 3)):
                    if exists(t):
                        stage(t, (u + (t - k)) % 2)

            h_cast(0, 0)
            for k in range(KC):
                act.wait_ge(w_in[0], 16 * KC)
                nc.scalar.activation(wh[0][:, k], wf[0][:, k], ACT.Copy, scale=UP).then_inc(w_high, 1)
            h_evict(0, 0)
            h_cast(1, 1)
            h_evict(1, 1)
            h_cast(2, 0)
            act.wait_ge(w_in[1], 16)
            nc.scalar.activation(wh[1][:], wf[1][:], ACT.Copy, scale=UP).then_inc(w_high, 1)
            slots(act, slot, 0, T + 1)

            def store(t, u, i, first):
                act.wait_ge(o_ready, t + 1)
                act.dma_start(out[t, :, :], y[:, u]).then_inc(stored[u], 16)

            over_tiles(act, store)
            for u in range(2):
                act.wait_ge(stored[u], 16 * (T // 2))

        @block.vector
        def _(dve):
            def h_low(t, u):
                dve.wait_ge(h_high, t + 1)
                nc.vector.tensor_tensor(hp[:, u, 1], ht[:, u], hp[:, u, 0], ALU.subtract).then_inc(h_split, 1)

            def biased(t, u):
                dve.wait_ge(mixed, t + 1)
                nc.vector.scalar_tensor_tensor(y[:, u], pm[u][:], 1.0 / UP, bias[:, 0, :], ALU.mult,
                                               ALU.add).then_inc(y_ready, 1)

            def elu(t, u):
                dve.wait_ge(y_exp, t + 1)
                nc.vector.tensor_scalar(y[:, u], y[:, u], 0.0, -1.0, ALU.max, ALU.add).then_inc(y_pos, 1)
                dve.wait_ge(y_pos, t + 1)
                nc.vector.tensor_tensor(ye[:, u], y[:, u], ye[:, u], ALU.add).then_inc(y_elu, 1)

            def stats(n, t, u, ready):
                dve.wait_ge(ready, t + 1)
                nc.vector.bn_stats(st[:, u], z[:, u]).then_inc(stats_ready, 1)
                dve.wait_ge(stats_ready, n + t + 1).then_inc(dve_passed, 1)
                nc.vector.bn_aggr(mv[:, u], st[:, u]).then_inc(var_ready, 1)

            def norm(n, t, u, dst, ready):
                dve.wait_ge(rstd_ready, n + t + 1)
                nc.vector.tensor_scalar(dst, z[:, u], mv[:, u, 0:1], rs[:, u], ALU.subtract,
                                        ALU.mult).then_inc(ready, 1)

            def x_low(t, u):
                dve.wait_ge(x_high, t + 1)
                nc.vector.tensor_tensor(xp[:, u, 1], x1[:, t, :], xp[:, u, 0], ALU.subtract).then_inc(x_split, 1)

            def s_low(t, u):
                dve.wait_ge(s_high, t + 1)
                nc.vector.tensor_tensor(sl[:, t, :], ps[u][:], sh[:, t, :], ALU.subtract).then_inc(s_split, 1)

            def slot(k, u):
                if exists(k):
                    biased(k, u)
                if exists(k - 1):
                    norm(0, k - 1, 1 - u, x1[:, k - 1, :], x1_ready)
                    x_low(k - 1, 1 - u)
                if exists(k):
                    elu(k, u)
                if exists(k - 2):
                    s_low(k - 2, u)
                if exists(k):
                    stats(0, k, u, z_ready)
                if exists(k + 3):
                    h_low(k + 3, 1 - u)

            nc.vector.reciprocal(rec[:], hid[:, :, :, DH]).then_inc(rec_ready, 1)
            h_low(0, 0)
            for k in range(KC):
                dve.wait_ge(w_high, k + 1)
                nc.vector.scalar_tensor_tensor(wl[0][:, k], wf[0][:, k], UP, wh[0][:, k], ALU.mult,
                                               ALU.subtract).then_inc(w_split, 1)
            h_low(1, 1)
            h_low(2, 0)
            dve.wait_ge(w_high, KC + 1)
            nc.vector.scalar_tensor_tensor(wl[1][:], wf[1][:], UP, wh[1][:], ALU.mult, ALU.subtract).then_inc(w_split, 1)
            dve.wait_ge(b_in, 32)
            slots(dve, slot, 0, T + 1)

            def second(t, u):
                dve.wait_ge(gathered, t + 1)
                dve.wait_ge(xb_ready, t + 1)
                nc.vector.scalar_tensor_tensor(z[:, u], po[u], 1.0 / UP, ye[:, u], ALU.mult,
                                               ALU.add).then_inc(o_sum, 1)

            def normed(t, u, i, first):
                second(t, u)
                stats(T, t, u, o_sum)
                if not first:
                    dve.wait_ge(stored[u], 16 * i)
                norm(T, t, u, y[:, u], o_ready)

            over_tiles(dve, normed)

        @block.tensor
        def _(pe):
            def product(to, parts, w, k):
                for q, (lhs, rhs) in enumerate(((0, wh[w]), (0, wl[w]), (1, wh[w]))):
                    last = nc.tensor.matmul(to[:], parts[:, lhs, k, :], rhs[:, k, :],
                                            start=(k == 0 and q == 0), stop=(k == KC - 1 and q == 2))
                return last

            def turn(rows, to):
                for w in range(2):
                    for k in range(KC):
                        last = nc.tensor.transpose(to[:, w, k, :], rows[:, w, k * P:(k + 1) * P], idb[:])
                return last

            def h_turn(t, u):
                pe.wait_ge(h_split, t + 1)
                if later(t):
                    pe.wait_ge(h_out, t - 1)
                turn(hp[:, u], ph[u]).then_inc(h_turned, 1)

            def mix(t, u):
                pe.wait_ge(h_out, t + 1)
                if later(t):
                    pe.wait_ge(y_ready, t - 1)
                for k in range(KC):
                    if isinstance(t, int) and t == 0:
                        pe.wait_ge(w_split, k + 1)
                    last = product(pm[u], h_t[:, u], 0, k)
                last.then_inc(mixed, 1)

            def x_turn(t, u):
                pe.wait_ge(x_split, t + 1)
                if later(t):
                    pe.wait_ge(x_out, t - 1)
                turn(xp[:, u], px[u]).then_inc(x_turned, 1)

            def support(t, u):
                pe.wait_ge(x_out, t + 1)
                if later(t):
                    pe.wait_ge(s_split, t - 1)
                if isinstance(t, int) and t == 0:
                    pe.wait_ge(w_split, KC + 1)
                for k in range(KC):
                    last = product(ps[u], x_t[:, u], 1, k)
                last.then_inc(supported, 1)

            def gather(u, js):
                for j in js:
                    for q, s in enumerate((sh, sl)):
                        last = nc.tensor.matmul(po[u], tile[u][:, j, :].bitcast(fp8), s[:, j, :],
                                                start=(j == 0 and q == 0), stop=(j == T - 1 and q == 1))
                return last

            def slot(k, u):
                for stage, t in ((mix, k), (h_turn, k + 2), (support, k - 2), (x_turn, k - 1)):
                    if exists(t):
                        stage(t, (u + (t - k)) % 2)

            pe.wait_ge(ident_ready, 1)
            h_turn(0, 0)
            h_turn(1, 1)
            slots(pe, slot, 0, T - 1)
            support(T - 2, 0)
            pe.wait_ge(tile_in[0], 16)
            pe.wait_ge(h_out, T)
            pe.wait_ge(s_split, T - 4)
            gather(0, range(0, T // 2))
            x_turn(T - 1, 1)
            gather(0, range(T // 2, T - 4))
            support(T - 1, 1)
            pe.wait_ge(s_split, T - 1)
            gather(0, range(T - 4, T - 1))
            pe.wait_ge(s_split, T)
            gather(0, range(T - 1, T)).then_inc(gathered, 1)
            pe.wait_ge(tile_in[1], 16)
            gather(1, range(T)).then_inc(gathered, 1)
            with pe.Fori(1, T // 2) as i:
                for u in range(2):
                    t = 2 * i + u
                    pe.wait_ge(tile_in[u], 16 * i + 16).then_inc(pe_passed, 1)
                    pe.wait_ge(o_sum, t - 1).then_inc(pe_passed, 1)
                    gather(u, range(T)).then_inc(gathered, 1)


def gat_gcn(nc, x, adj, w_seq, a1, a2, w_out, b_out, w1, b1, out):
    s1_rows = nc.dram_tensor("s1_rows", [H, N], fp32, kind="Internal").ap()
    x_t = x.rearrange("(t p) d -> t p d", p=P)
    adj_t = adj.rearrange("(t p) n -> t p n", p=P)
    out_t = out.rearrange("(t p) d -> t p d", p=P)
    with ExitStack() as ctx:
        adjT = ctx.enter_context(nc.sbuf_tensor("adjT", [P, T, T, P], u8))
        hid = ctx.enter_context(nc.sbuf_tensor("hid", [P, T, H, C], fp32))
        with ExitStack() as mid:
            AB = mid.enter_context(nc.sbuf_tensor("AB", [P, T, 2, H], fp32))
            S2 = mid.enter_context(nc.sbuf_tensor("S2", [P, H, 2, T], fp32))
            V = mid.enter_context(nc.sbuf_tensor("V", [P, H, T, CW], fp16))
            project_nodes(nc, x_t, adj_t, w_seq, a1, a2, s1_rows, adjT, hid, V, AB, S2)
            attend(nc, s1_rows, adjT, V, AB, S2, hid)
        finish(nc, x_t, w_out, b_out, w1, b1, out_t, adjT, hid)


_INS = ['x', 'adj', 'L0_gnn_W_seq', 'L0_gnn_a1', 'L0_gnn_a2', 'L0_gnn_W_out', 'L0_gnn_b_out',
        'L1_gnn_weight', 'L1_gnn_bias']
_OUTS = [((2048, 512), 'float32')]


def kernel(**inputs):
    import numpy as _np
    import concourse.bacc as _bacc
    from concourse import mybir as _mybir
    from concourse.bass_utils import run_bass_kernel_spmd as _run

    nc = _bacc.Bacc("TRN2", target_bir_lowering=False, num_devices=1)
    arrays, args = {}, []
    for name in _INS:
        a = _np.ascontiguousarray(inputs[name])
        arrays[f"in_{name}_dram"] = a
        args.append(nc.dram_tensor(f"in_{name}_dram", a.shape, _mybir.dt.from_np(a.dtype), kind="ExternalInput").ap())
    for i, (shape, dtype) in enumerate(_OUTS):
        dt = _mybir.dt.from_np(_np.dtype(dtype))
        args.append(nc.dram_tensor(f"out_{i}_dram", shape, dt, kind="ExternalOutput").ap())
    gat_gcn(nc, *args)
    r = _run(nc, [arrays], core_ids=[0])
    return r.results[0]["out_0_dram"]
```

```python
import concourse.bass as bass
from concourse import mybir
from contextlib import ExitStack

P = 128
N = 2048
D = 512
H = 16
DH = D // H
T = N // P
KC = D // P
HALVES = 2
TH = T // HALVES
NH = N // HALVES
C = DH + 1
CV = 2 * C
CW = 2 * CV
PAIRS = H // 2
CH = 4
NCH = T // CH
BANK = 512
TB = BANK // CW
AG = [(0, 6), (6, 11), (11, 16)]
SLOPE = 0.2
STEEP = 2.0 ** 40
UP = 64.0
FP8_ONE = 56
EPS = 1e-5

fp32, fp16, bf16 = mybir.dt.float32, mybir.dt.float16, mybir.dt.bfloat16
fp8, u8, u32 = mybir.dt.float8e4, mybir.dt.uint8, mybir.dt.uint32
ALU = mybir.AluOpType
ACT = mybir.ActivationFunctionType
AX = mybir.AxisListType


def spread(ap, shape):
    return ap.to_broadcast(shape)


def project_nodes(nc, x, adj, w, a1, a2, s1_rows, adjT, hid, V, AB, S2, s1b, s2c, shared):
    ctx = ExitStack()
    with ctx:
        def sb(name, shape, dt):
            return ctx.enter_context(nc.sbuf_tensor(name, shape, dt))

        def pb(name, shape, dt):
            return ctx.enter_context(nc.psum_tensor(name, shape, dt))

        def sem(name):
            return ctx.enter_context(nc.semaphore(name))

        WX = D + 2 * H
        at = shared.bitcast(fp32).rearrange("p (u n) -> p u n", u=2)
        XB = 2
        NB = T // XB
        ab = sb("ab", [P, 2, N], fp16)
        parts = hid[:].rearrange("p t h c -> p (t h c)").bitcast(fp16)[:, 0:2 * T * D].rearrange(
            "p (w t k n) -> p w t k n", w=2, t=T, k=KC)
        xh, xl = parts[:, 0], parts[:, 1]
        wf = sb("wf", [P, KC, WX], fp32)
        wp = sb("wp", [P, 2, H, DH], fp32)
        wh = sb("wh", [P, KC, WX], fp16)
        wl = sb("wl", [P, KC, WX], fp16)
        av = sb("av", [P, 2, DH], fp32)
        sc = sb("sc", [P, T, 2, H], fp32)
        Vf = V[:].rearrange("p h t c -> p (h t c)")
        XE = XB * D
        xr = Vf[:, 0:4 * XE].rearrange("p (u w q d) -> p u w q d", u=2, w=2, q=XB)
        srow = Vf[0:2 * H, 4 * XE:4 * XE + 2 * N].bitcast(fp32)
        xt = Vf[:, 4 * XE + 2 * N:4 * XE + 2 * N + 2 * T * D].bitcast(fp32).rearrange("p (t d) -> p t d", t=T)
        RB = BANK // P
        bmx = sb("bmx", [2 * H, T // RB], fp32)
        gmx = sb("gmx", [2 * H, 1], fp32)
        grow = sb("grow", [1, 2 * H], fp32)
        ones = sb("ones", [1, P], fp32)
        ones_col = sb("ones_col", [P, 1], fp32)
        warm = sb("warm", [P, 1], fp32)
        G = sb("G", [P, 2 * H], fp32)
        tt = sb("tt", [P, T, H], fp32)
        lr = sb("lr", [P, T, H], fp32)
        ea = sb("ea", [P, 2, T, H], fp32)
        F = sb("F", [P, 2, T, H], fp32)
        vt = wf[:].rearrange("p k n -> p (k n)")[:, 0:2 * H * CV].rearrange("p (u h a c) -> p u h a c", u=2, h=H, a=2)
        idf = sb("idf", [P, P], fp32)
        idb = sb("idb", [P, P], fp16)
        pxt = [pb(f"pxt{u}", [P, 2, KC, P], fp16) for u in range(2)]
        psq = [pb(f"psq{u}", [P, D], fp32) for u in range(2)]
        psc = [pb(f"psc{u}", [P, T * 2 * H], fp32) for u in range(2)]
        pat = [pb(f"pat{u}", [P, TH, P], fp16) for u in range(2)]
        rows = [p[0:2 * H, :] for p in (*psq, *psc)]

        w_loaded = [sem(f"w_loaded{k}") for k in range(KC)]
        a_loaded = sem("a_loaded")
        x_loaded = [sem(f"x_loaded{b}") for b in range(NB)]
        adj_loaded = [sem(f"adj_loaded{u}") for u in range(2)]
        ones_set = sem("ones_set")
        ident_ready = sem("ident_ready")
        w_prod = sem("w_prod")
        w_step = sem("w_step")
        w_high = sem("w_high")
        w_split = sem("w_split")
        wa_high = sem("wa_high")
        wa_split = sem("wa_split")
        x_turned = sem("x_turned")
        x_cast = sem("x_cast")
        x_split = sem("x_split")
        even_out = sem("even_out")
        odd_out = sem("odd_out")
        scored = sem("scored")
        row_out = sem("row_out")
        bank_max = sem("bank_max")
        nodes_turned = sem("nodes_turned")
        sc_ready = sem("sc_ready")
        row_max = sem("row_max")
        max_turned = sem("max_turned")
        max_row = sem("max_row")
        max_spread = sem("max_spread")
        g_ready = sem("g_ready")
        row_stored = sem("row_stored")
        e_step = sem("e_step")
        s2_ready = sem("s2_ready")
        heads_in = sem("heads_in")
        exp_in = sem("exp_in")
        exp_out = sem("exp_out")
        edges_cast = sem("edges_cast")
        adj_turned = sem("adj_turned")
        adj_out = sem("adj_out")
        projected = sem("projected")
        scaled = sem("scaled")
        v_high = sem("v_high")
        v_split = sem("v_split")
        pool_passed = sem("pool_passed_a")

        block = ctx.enter_context(nc.Block())

        @block.sync
        def _(sp):
            sp.dma_start(av[:, 0, :], a1[None, :].to_broadcast([P, DH])).then_inc(a_loaded, 16)
            sp.dma_start(av[:, 1, :], a2[None, :].to_broadcast([P, DH])).then_inc(a_loaded, 16)
            for b in range(NB):
                sp.dma_start(xt[:, b * XB:(b + 1) * XB, :],
                             x[b * XB:(b + 1) * XB, :, :].rearrange("q p d -> p q d")).then_inc(x_loaded[b], 16)
                if b < KC:
                    sp.dma_start(wf[:, b, 0:D], w[b * P:(b + 1) * P, :]).then_inc(w_loaded[b], 16)

            def load(t, u, first):
                if not first:
                    sp.wait_ge(edges_cast, t - 1)
                sp.dma_start(at[:, u, :], adj[t, :, :]).then_inc(adj_loaded[u], 16)

            for t in range(4):
                load(t, t % 2, t < 2)
            sp.wait_ge(row_out, T // RB)
            sp.dma_start(s1_rows[:, :], srow[0:H, :]).then_inc(row_stored, 16)
            with sp.Fori(2, T // 2) as i:
                for u in range(2):
                    load(2 * i + u, u, False)
            sp.wait_ge(row_stored, 16)
            sp.wait_ge(s2_ready, 2)
            for a in range(2):
                sp.dma_start(s1b[a], s1_rows[a:a + 1, 0:NH].to_broadcast([P, NH])).then_inc(heads_in, 16)
                sp.dma_start(s2c[a][:], S2[:, a, :, :]).then_inc(heads_in, 16)
            sp.wait_ge(heads_in, 64)

        @block.gpsimd
        def _(pool):
            nc.gpsimd.memset(idf[:], 1.0).then_inc(ones_set, 1)
            nc.gpsimd.memset(idb[:], 1.0).then_inc(ones_set, 1)
            nc.gpsimd.memset(ones[:], 1.0).then_inc(ones_set, 1)
            nc.gpsimd.memset(ones_col[:], 1.0).then_inc(ones_set, 1)
            pool.wait_ge(ones_set, 4)
            for m in (idf, idb):
                nc.gpsimd.affine_select(out=m[:], in_=m[:], compare_op=ALU.is_equal, fill=0.0, base=0,
                                        pattern=[[-1, P]], channel_multiplier=1).then_inc(ident_ready, 1)
            pool.wait_ge(a_loaded, 32)
            for k in range(KC):
                pool.wait_ge(w_loaded[k], 16)
                for s in range(2):
                    if k:
                        pool.wait_ge(w_step, 2 * k + s - 1)
                    nc.gpsimd.tensor_tensor(wp[:, s], wf[:, k, 0:D].rearrange("p (h d) -> p h d", h=H),
                                            spread(av[:, s:s + 1, :], [P, H, DH]), ALU.mult).then_inc(w_prod, 1)

            def low(t, u):
                pool.wait_ge(v_high, t + 1).then_inc(pool_passed, 1)
                nc.gpsimd.tensor_tensor(V[:, :, t, CV:CW], vt[:, u].rearrange("p h a c -> p h (a c)"),
                                        V[:, :, t, 0:CV], ALU.subtract).then_inc(v_split, 1)

            with pool.Fori(0, T // 2 - 1) as i:
                for u in range(2):
                    low(2 * i + u, u)
            low(T - 2, 0)

        @block.scalar
        def _(act):
            def cut(b):
                act.wait_ge(x_loaded[b], 16)
                if b >= 2:
                    act.wait_ge(x_turned, XB * (b - 1))
                nc.scalar.activation(xr[:, b % 2, 0], xt[:, b * XB:(b + 1) * XB, :], ACT.Copy).then_inc(x_cast, 1)

            def edges_out(t):
                for f in range(2):
                    act.wait_ge(adj_turned, 2 * t + f + 1)
                    nc.scalar.activation(adjT[:, t, f * TH:(f + 1) * TH, :], pat[f][:], ACT.Copy,
                                         scale=float(FP8_ONE)).then_inc(adj_out, 1)

            def high(t, u):
                act.wait_ge(scaled, 2 * t + 2)
                nc.scalar.activation(V[:, :, t, 0:CV], vt[:, u].rearrange("p h a c -> p h (a c)"),
                                     ACT.Copy).then_inc(v_high, 1)

            def row_evict(b):
                act.wait_ge(scored, b + 1)
                nc.scalar.activation(srow[:, b * BANK:(b + 1) * BANK], rows[b], ACT.Copy,
                                     scale=1.0 / UP).then_inc(row_out, 1)

            cut(0)
            cut(1)
            for b in range(NB):
                t = XB * b
                act.wait_ge(x_turned, t + 1)
                nc.scalar.activation(parts[:, :, t].rearrange("p w k n -> p w (k n)"),
                                     pxt[0][:].rearrange("p w k n -> p w (k n)"), ACT.Copy).then_inc(even_out, 1)
                if b + 2 < NB:
                    cut(b + 2)
                if b == KC:
                    act.wait_ge(w_step, 2 * KC)
                    nc.scalar.activation(wh[:, :, D:WX], wf[:, :, D:WX], ACT.Copy, scale=UP).then_inc(wa_high, 1)
                if b == NB - 3:
                    nc.scalar.activation(wh[:, :, 0:D], wf[:, :, 0:D], ACT.Copy, scale=UP).then_inc(w_high, 1)
                if b >= NB - 3:
                    row_evict(b - (NB - 3))
            row_evict(3)
            edges_out(0)
            act.wait_ge(exp_in, 1)
            nc.scalar.activation(F[:, 0], tt[:], ACT.Exp).then_inc(exp_out, 1)
            nc.scalar.activation(F[:, 1], tt[:], ACT.Exp, scale=SLOPE).then_inc(exp_out, 1)
            edges_out(1)
            edges_out(2)
            act.wait_ge(e_step, 4)
            nc.scalar.activation(ea[:], ea[:], ACT.Exp).then_inc(exp_out, 1)
            act.wait_ge(ones_set, 4)
            nc.scalar.activation(warm[:], ones_col[:], ACT.Sigmoid)
            act.wait_ge(row_stored, 16)
            with act.Fori(0, T // 2 - 2) as i:
                for u in range(2):
                    edges_out(2 * i + u + 3)
                    high(2 * i + u, u)
            edges_out(T - 1)
            for t in range(T - 4, T):
                high(t, t % 2)

        @block.vector
        def _(dve):
            for n, free in enumerate((even_out, odd_out)):
                nc.vector.memset(G[:, n:n + 1], 0.0).then_inc(free, 1)

            def cut(b):
                dve.wait_ge(x_cast, b + 1)
                if b >= 2:
                    dve.wait_ge(x_turned, XB * (b - 1))
                nc.vector.tensor_tensor(xr[:, b % 2, 1], xt[:, b * XB:(b + 1) * XB, :], xr[:, b % 2, 0],
                                        ALU.subtract).then_inc(x_split, 1)

            def split(c0, c1, high, done):
                dve.wait_ge(high, 1)
                nc.vector.scalar_tensor_tensor(wl[:, :, c0:c1], wf[:, :, c0:c1], UP, wh[:, :, c0:c1],
                                               ALU.mult, ALU.subtract).then_inc(done, 1)

            def cast(t, u, i, first):
                dve.wait_ge(adj_loaded[u], 16 * i + 16)
                if not first:
                    dve.wait_ge(adj_turned, 2 * t - 2)
                nc.vector.tensor_copy(ab[:, u], at[:, u]).then_inc(edges_cast, 1)

            def row_max_of(b):
                dve.wait_ge(row_out, b + 1)
                nc.vector.tensor_reduce(bmx[:, b:b + 1], srow[:, b * BANK:(b + 1) * BANK], AX.X,
                                        ALU.max).then_inc(bank_max, 1)

            cut(0)
            cut(1)
            for b in range(NB):
                t = XB * b + 1
                dve.wait_ge(x_turned, t + 1)
                nc.vector.tensor_copy(parts[:, :, t], pxt[1][:]).then_inc(odd_out, 1)
                if b + 2 < NB:
                    cut(b + 2)
                if b < KC:
                    for s in range(2):
                        dve.wait_ge(w_prod, 2 * b + s + 1)
                        nc.vector.tensor_reduce(wf[:, b, D + s * H:D + (s + 1) * H], wp[:, s], AX.X,
                                                ALU.add).then_inc(w_step, 1)
                if b == KC:
                    split(D, WX, wa_high, wa_split)
                if b == NB - 3:
                    split(0, D, w_high, w_split)
                if b >= NB - 2:
                    row_max_of(b - (NB - 2))
                    cast(b - (NB - 2), b - (NB - 2), 0, True)
            row_max_of(2)
            row_max_of(3)
            dve.wait_ge(bank_max, T // RB)
            nc.vector.tensor_reduce(gmx[:], bmx[:], AX.X, ALU.max).then_inc(row_max, 1)
            dve.wait_ge(max_turned, 1)
            nc.vector.tensor_copy(grow[:], psc[1][0:1, 0:2 * H]).then_inc(max_row, 1)
            dve.wait_ge(nodes_turned, 1)
            nc.vector.tensor_copy(sc[:].rearrange("p t s h -> p (t s h)"), psc[0][:]).then_inc(sc_ready, 1)
            dve.wait_ge(sc_ready, 1)
            nc.vector.tensor_scalar(S2[:, :, 0, :], sc[:, :, 1, :].rearrange("p t h -> p h t"), -1.0, None,
                                    ALU.mult).then_inc(s2_ready, 1)
            nc.vector.tensor_scalar(S2[:, :, 1, :], sc[:, :, 1, :].rearrange("p t h -> p h t"), STEEP, None,
                                    ALU.mult).then_inc(s2_ready, 1)
            dve.wait_ge(max_spread, 1)
            nc.vector.tensor_copy(G[:], psc[1][:, 0:2 * H]).then_inc(g_ready, 1)
            dve.wait_ge(g_ready, 1)
            g = spread(G[:, None, H:2 * H], [P, T, H])
            nc.vector.tensor_tensor(tt[:], sc[:, :, 1, :], g, ALU.subtract).then_inc(exp_in, 1)
            cast(2, 0, 1, False)
            dve.wait_ge(exp_out, 2)
            nc.vector.tensor_tensor(tt[:], sc[:, :, 0, :], g, ALU.add).then_inc(e_step, 1)
            dve.wait_ge(e_step, 1)
            nc.vector.scalar_tensor_tensor(lr[:], tt[:], SLOPE, tt[:], ALU.mult, ALU.max).then_inc(e_step, 1)
            dve.wait_ge(e_step, 2)
            nc.vector.tensor_tensor(ea[:, 0], tt[:], lr[:], ALU.subtract).then_inc(e_step, 1)
            nc.vector.scalar_tensor_tensor(ea[:, 1], tt[:], SLOPE, lr[:], ALU.mult, ALU.subtract).then_inc(e_step, 1)
            def weigh(t, u, first):
                dve.wait_ge(projected, t + 1)
                if not first:
                    dve.wait_ge(v_split, t - 1)
                nc.vector.tensor_tensor(vt[:, u, :, :, 0:DH],
                                        spread(psq[u][:].rearrange("p (h d) -> p h d", h=H)[:, :, None, :],
                                               [P, H, 2, DH]),
                                        spread(F[:, :, t, :].rearrange("p a h -> p h a")[:, :, :, None],
                                               [P, H, 2, DH]), ALU.mult).then_inc(scaled, 1)
                nc.vector.tensor_scalar(vt[:, u, :, :, DH], F[:, :, t, :].rearrange("p a h -> p h a"), UP, None,
                                        ALU.mult).then_inc(scaled, 1)

            cast(3, 1, 1, False)
            weigh(0, 0, True)
            dve.wait_ge(exp_out, 3)
            nc.vector.tensor_copy(AB[:, :, 0, :], ea[:, 0])
            nc.vector.tensor_scalar(AB[:, :, 1, :], ea[:, 1], -1.0, None, ALU.mult)
            cast(4, 0, 2, False)
            weigh(1, 1, True)
            with dve.Fori(1, T // 2 - 2) as i:
                cast(2 * i + 3, 1, i + 1, False)
                weigh(2 * i, 0, False)
                cast(2 * i + 4, 0, i + 2, False)
                weigh(2 * i + 1, 1, False)
            cast(T - 1, 1, T // 2 - 1, False)
            for t in range(T - 4, T):
                weigh(t, t % 2, False)
            dve.wait_ge(v_high, T)
            nc.vector.tensor_tensor(V[:, :, T - 1, CV:CW], vt[:, 1].rearrange("p h a c -> p h (a c)"),
                                    V[:, :, T - 1, 0:CV], ALU.subtract)

        @block.tensor
        def _(pe):
            PARTS = ((xh, wh), (xh, wl), (xl, wh))
            pe.wait_ge(ident_ready, 2)

            def x_turn(b, v, n):
                pe.wait_ge(x_split, b + 1)
                for q in range(XB):
                    pe.wait_ge((even_out, odd_out)[q], n + 1)
                    for w in range(2):
                        for k in range(KC):
                            last = nc.tensor.transpose(pxt[q][:, w, k, :], xr[:, v, w, q, k * P:(k + 1) * P], idb[:])
                    last.then_inc(x_turned, 1)

            def score(b):
                pe.wait_ge(even_out, 1 + RB // 2 * (b + 1))
                pe.wait_ge(odd_out, 1 + RB // 2 * (b + 1))
                for k in range(KC):
                    for m, (lhs, rhs) in enumerate(PARTS):
                        last = nc.tensor.matmul(rows[b], rhs[:, k, D:WX], lhs[:, b * RB:(b + 1) * RB, k, :],
                                                start=(k == 0 and m == 0), stop=(k == KC - 1 and m == 2))
                last.then_inc(scored, 1)

            def turn_edges(t, u, very_first):
                pe.wait_ge(edges_cast, t + 1)
                for f in range(2):
                    if not very_first:
                        pe.wait_ge(adj_out, 2 * t + f - 1)
                    for b in range(TH):
                        c = (f * TH + b) * P
                        last = nc.tensor.transpose(pat[f][:, b, :], ab[:, u, c:c + P], idb[:])
                    last.then_inc(adj_turned, 1)

            with pe.Fori(0, (NB - 2) // 2) as i:
                for v in range(2):
                    x_turn(2 * i + v, v, 2 * i + v)
            pe.wait_ge(wa_split, 1)
            score(0)
            x_turn(NB - 2, 0, NB - 2)
            score(1)
            x_turn(NB - 1, 1, NB - 1)
            score(2)
            score(3)
            turn_edges(0, 0, True)

            def project(t, u, first):
                if not first:
                    pe.wait_ge(scaled, 2 * t - 2)
                for k in range(KC):
                    for m, (lhs, rhs) in enumerate(PARTS):
                        last = nc.tensor.matmul(psq[u][:], lhs[:, t, k, :], rhs[:, k, 0:D],
                                                start=(k == 0 and m == 0), stop=(k == KC - 1 and m == 2))
                last.then_inc(projected, 1)

            pe.wait_ge(row_out, T // RB)
            for t in range(T):
                last = nc.tensor.transpose(psc[0][:, t * 2 * H:(t + 1) * 2 * H], srow[:, t * P:(t + 1) * P],
                                           idf[0:2 * H, 0:2 * H])
            last.then_inc(nodes_turned, 1)
            pe.wait_ge(row_max, 1)
            nc.tensor.transpose(psc[1][0:1, 0:2 * H], gmx[:], idf[0:2 * H, 0:2 * H]).then_inc(max_turned, 1)
            turn_edges(1, 1, False)
            pe.wait_ge(max_row, 1)
            nc.tensor.matmul(psc[1][:, 0:2 * H], ones[:], grow[:], start=True, stop=True).then_inc(max_spread, 1)
            pe.wait_ge(w_split, 1)
            project(0, 0, True)
            turn_edges(2, 0, False)
            project(1, 1, True)
            turn_edges(3, 1, False)
            with pe.Fori(1, T // 2 - 1) as i:
                for u in range(2):
                    turn_edges(2 * i + u + 2, u, False)
                    project(2 * i + u, u, False)
            project(T - 2, 0, False)
            project(T - 1, 1, False)


def attend(nc, s1_rows, w_out, adjT, V, AB, S2, s1b, s2c, shared, hid, ahead):
    ctx = ExitStack()
    with ctx:
        def sb(name, shape, dt):
            return ctx.enter_context(nc.sbuf_tensor(name, shape, dt))

        def pb(name, shape, dt):
            return ctx.enter_context(nc.psum_tensor(name, shape, dt))

        def sem(name):
            return ctx.enter_context(nc.semaphore(name))

        edge = [shared.rearrange("p (t n) -> p t n", t=T), sb("edge1", [P, T, NH], u8)]
        vcur = [sb(f"vcur{a}", [P, T, CW], fp16) for a in range(2)]
        tile = sb("tile", [P, T, P], u8)
        esum = [sb(f"esum{a}", [P, TH, CW], fp32) for a in range(2)]
        asum = sb("asum", [P, H, CV], fp32)
        pair = sb("pair", [P, TH, 2, C], fp32)
        plain = sb("plain", [P, H, C], fp32)
        pe_e = [pb(f"pe_e{a}", [P, 3, BANK], fp32) for a in range(2)]
        pe_a = [pb(f"pe_a{b}", [P, BANK], fp32) for b in range(2)]

        head_in = [sem(f"head_in{a}") for a in range(2)]
        v_in = [sem(f"v_in{a}") for a in range(2)]
        tile_in = sem("tile_in")
        act_passed = sem("act_passed")
        pe_passed = sem("pe_passed")
        pool_passed = sem("pool_passed")
        dve_passed = sem("dve_passed_b")
        act_sign = sem("act_sign")
        dve_sign = sem("dve_sign")
        masked = sem("masked")
        head_done = sem("head_done")
        plain_done = sem("plain_done")
        head_out = sem("head_out")
        plain_out = sem("plain_out")
        joined = sem("joined")
        joined_a = sem("joined_a")
        p_step = sem("p_step")
        q_step = sem("q_step")

        ITER = HALVES * PAIRS
        assert ITER == T

        def join(eng, ops, passed, g, half, h, a):
            eng.wait_ge(head_out, 2 * g + 2)
            ops.tensor_tensor(pair[:].rearrange("p t s c -> p t (s c)"), esum[a][:, :, 0:CV],
                              esum[a][:, :, CV:CW], ALU.add).then_inc(joined, 1)
            eng.wait_ge(joined, g + 2).then_inc(passed, 1)
            ops.tensor_tensor(pair[:], pair[:], spread(AB[:, half * TH:(half + 1) * TH, :, bass.ds(h, 1)],
                                                       [P, TH, 2, C]), ALU.mult).then_inc(p_step, 1)
            for s in range(2):
                eng.wait_ge(p_step, 3 * g + s + 1).then_inc(passed, 1)
                ops.tensor_tensor(hid[:, half * TH:(half + 1) * TH, h, :],
                                  hid[:, half * TH:(half + 1) * TH, h, :], pair[:, :, s, :],
                                  ALU.add).then_inc(p_step, 1)
            eng.wait_ge(p_step, 3 * g + 3)

        block = ctx.enter_context(nc.Block())

        @block.sync
        def _(sp):
            def load(it, half, p, first):
                for a in range(2):
                    g = 2 * it + a
                    if not first:
                        sp.wait_ge(masked, NCH * (g - 1))
                        sp.dma_start(s1b[a], s1_rows[bass.ds(2 * p + a, 1), bass.ds(half * NH, NH)]
                                     .to_broadcast([P, NH])).then_inc(head_in[a], 16)
                        sp.dma_start(s2c[a][:], S2[:, 2 * p + a, :, :]).then_inc(head_in[a], 16)
                        sp.wait_ge(head_done, g - 1)
                    sp.dma_start(vcur[a][:], V[:, 2 * p + a, :, :]).then_inc(v_in[a], 16)
                    if a == 0 and not first:
                        sp.wait_ge(plain_done, 3 * it)
                        sp.dma_start(tile[:], adjT[:, it, :, :]).then_inc(tile_in, 16)

            load(0, 0, 0, True)
            with sp.Fori(1, PAIRS) as p:
                load(p, 0, p, False)
            with sp.Fori(0, PAIRS) as p:
                load(p + PAIRS, 1, p, False)
            sp.wait_ge(masked, NCH * 2 * ITER)
            for k in range(KC):
                sp.dma_start(ahead.wf[:, k], w_out[k * P:(k + 1) * P, :]).then_inc(ahead.w_in[k], 16)
            for k in range(KC):
                sp.wait_ge(ahead.w_in[k], 16)

        @block.scalar
        def _(act):
            def evict(g, a, first):
                act.wait_ge(head_done, g + 1)
                if not first:
                    act.wait_ge(joined, g)
                nc.scalar.activation(esum[a][:, 0:2 * TB, :].rearrange("p (b t) c -> p b (t c)", b=2),
                                     pe_e[a][:, 0:2, 0:TB * CW], ACT.Copy).then_inc(head_out, 1)
                nc.scalar.activation(esum[a][:, 2 * TB:TH, :].rearrange("p t c -> p (t c)"),
                                     pe_e[a][:, 2, 0:(TH - 2 * TB) * CW], ACT.Copy).then_inc(head_out, 1)

            def slots(it, first):
                for a in range(2):
                    g = 2 * it + a
                    if not first:
                        act.wait_ge(head_in[a], 32 * it)
                        act.wait_ge(head_done, g - 1).then_inc(act_passed, 1)
                    for c in range(NCH):
                        for j in range(CH * c + CH // 2, CH * (c + 1)):
                            ins = nc.scalar.activation(edge[a][:, j, :].bitcast(fp8), s1b[a], ACT.Sigmoid,
                                                       bias=s2c[a][:, 1, j:j + 1], scale=STEEP, saturate=False)
                        ins.then_inc(act_sign, 1)
                    if not (first and a == 0):
                        evict(g - 1, 1 - a, first)

            slots(0, True)
            with act.Fori(1, ITER) as it:
                slots(it, False)
            act.wait_ge(head_done, 2 * ITER - 1)
            for k in range(KC):
                act.wait_ge(ahead.w_in[k], 16)
                nc.scalar.activation(ahead.wh[:, k], ahead.wf[:, k], ACT.Copy, scale=UP).then_inc(ahead.w_high, 1)
            for u in range(2):
                act.wait_ge(ahead.h_ready, u + 1)
                nc.scalar.activation(ahead.hp[:, u, 0], ahead.ht[:, u], ACT.Copy).then_inc(ahead.h_high, 1)
            evict(2 * ITER - 1, 1, False)

        @block.vector
        def _(dve):
            def evict_plain(n, k):
                h0, h1 = AG[k]
                dve.wait_ge(plain_done, n + 1)
                nc.vector.tensor_copy(asum[:, h0:h1, :].rearrange("p h c -> p (h c)"),
                                      pe_a[k % 2][:, 0:(h1 - h0) * CV]).then_inc(plain_out, 1)

            def slots(it, half, first):
                for a in range(2):
                    g = 2 * it + a
                    if not first:
                        dve.wait_ge(head_in[a], 32 * it)
                        dve.wait_ge(head_done, g - 1)
                    elif a == 1:
                        evict_plain(0, 0)

                    def sign(c):
                        for j in range(CH * c, CH * c + CH // 2):
                            ins = nc.vector.tensor_scalar(edge[a][:, j, :], s1b[a], s2c[a][:, 0, j:j + 1],
                                                          float(FP8_ONE), ALU.is_gt, ALU.mult)
                        ins.then_inc(dve_sign, 1)

                    sign(0)
                    for c in range(NCH):
                        if c + 1 < NCH:
                            sign(c + 1)
                        dve.wait_ge(act_sign, NCH * g + c + 1)
                        dve.wait_ge(dve_sign, NCH * g + c + 1)
                        e = edge[a][:, CH * c:CH * (c + 1), :].rearrange("p j (t i) -> p j t i", t=TH).bitcast(u32)
                        m = adjT[:, half * TH:(half + 1) * TH, CH * c:CH * (c + 1), :].rearrange(
                            "p t j i -> p j t i").bitcast(u32)
                        nc.vector.tensor_tensor(e, e, m, ALU.bitwise_and).then_inc(masked, 1)
                        if c == 1 and a == 0 and not first:
                            evict_plain(3 * it - 2, 1)
                            evict_plain(3 * it - 1, 2)
                        if c == 2 and a == 1 and not first:
                            dve.wait_ge(joined_a, it)
                            evict_plain(3 * it, 0)

            slots(0, 0, True)
            with dve.Fori(1, PAIRS) as p:
                slots(p, 0, False)
            with dve.Fori(0, PAIRS) as p:
                slots(p + PAIRS, 1, False)
            evict_plain(3 * ITER - 2, 1)
            evict_plain(3 * ITER - 1, 2)
            dve.wait_ge(joined, 1 + 2 * ITER - 1)
            nc.vector.reciprocal(ahead.rec[:, 0:TH], hid[:, 0:TH, :, DH]).then_inc(ahead.rec_ready, 1)
            dve.wait_ge(head_done, 2 * ITER - 1)
            for k in range(KC):
                dve.wait_ge(ahead.w_high, k + 1)
                nc.vector.scalar_tensor_tensor(ahead.wl[:, k], ahead.wf[:, k], UP, ahead.wh[:, k], ALU.mult,
                                               ALU.subtract).then_inc(ahead.w_split, 1)
            for u in range(2):
                dve.wait_ge(ahead.h_high, u + 1)
                nc.vector.tensor_tensor(ahead.hp[:, u, 1], ahead.ht[:, u], ahead.hp[:, u, 0],
                                        ALU.subtract).then_inc(ahead.h_split, 1)
            dve.wait_ge(p_step, 3 * (2 * H - 1))
            dve.wait_ge(q_step, 2 * T)
            join(dve, nc.vector, dve_passed, 2 * H - 1, 1, H - 1, 1)

        @block.tensor
        def _(pe):
            def plain_sum(it, k, first):
                h0, h1 = AG[k]
                if k == 2 or not first:
                    pe.wait_ge(plain_out, 3 * it + (0, -1, 1)[k]).then_inc(pe_passed, 1)
                if k == 0 and not first:
                    pe.wait_ge(tile_in, 16 * it).then_inc(pe_passed, 1)
                edges = adjT[:, 0] if first else tile[:]
                for j in range(T):
                    ins = nc.tensor.matmul(pe_a[k % 2][:, 0:(h1 - h0) * CV], edges[:, j, :].bitcast(fp8),
                                           V[:, h0:h1, j, :].rearrange("p h (w c) -> p h w c", w=2)[:, :, :, C:CV],
                                           start=(j == 0), stop=(j == T - 1))
                ins.then_inc(plain_done, 1)

            def slots(it, first):
                for a in range(2):
                    g = 2 * it + a
                    for k in ((0,), (1, 2))[a]:
                        plain_sum(it, k, first)
                    pe.wait_ge(v_in[a], 16 * it + 16)
                    if not first:
                        pe.wait_ge(head_out, 2 * g - 2)
                    for c in range(NCH):
                        pe.wait_ge(masked, NCH * g + c + 1).then_inc(pe_passed, 1)
                        for j in range(CH * c, CH * (c + 1)):
                            for i in range(TH):
                                b, o = i // TB, (i % TB) * CW
                                ins = nc.tensor.matmul(pe_e[a][:, b, o:o + CW],
                                                       edge[a][:, j, i * P:(i + 1) * P].bitcast(fp8), vcur[a][:, j, :],
                                                       start=(j == 0 and i % TB == 0), stop=(j == T - 1),
                                                       skip_group_check=True)
                    ins.then_inc(head_done, 1)

            slots(0, True)
            with pe.Fori(1, ITER) as it:
                slots(it, False)

        @block.gpsimd
        def _(pool):
            nc.gpsimd.memset(hid[:], 0.0).then_inc(joined, 1)
            pool.wait_ge(joined, 1)

            def join_head(*head):
                join(pool, nc.gpsimd, pool_passed, *head)

            def join_plain(t):
                pool.wait_ge(plain_out, 3 * t + 3)
                nc.gpsimd.tensor_tensor(plain[:], asum[:, :, 0:C], asum[:, :, C:CV], ALU.add).then_inc(joined_a, 1)
                pool.wait_ge(joined_a, t + 1).then_inc(pool_passed, 1)
                nc.gpsimd.tensor_tensor(plain[:], plain[:], spread(AB[:, t, 1, :][:, :, None], [P, H, C]),
                                        ALU.mult).then_inc(q_step, 1)
                pool.wait_ge(q_step, 2 * t + 1).then_inc(pool_passed, 1)
                nc.gpsimd.tensor_tensor(hid[:, t], hid[:, t], plain[:], ALU.subtract).then_inc(q_step, 1)
                pool.wait_ge(q_step, 2 * t + 2)

            join_head(0, 0, 0, 0)
            with pool.Fori(1, PAIRS) as p:
                join_head(2 * p - 1, 0, 2 * p - 1, 1)
                join_plain(p - 1)
                join_head(2 * p, 0, 2 * p, 0)
            join_head(H - 1, 0, H - 1, 1)
            join_plain(PAIRS - 1)
            join_head(H, 1, 0, 0)
            with pool.Fori(1, PAIRS) as p:
                join_head(H + 2 * p - 1, 1, 2 * p - 1, 1)
                join_plain(PAIRS + p - 1)
                join_head(H + 2 * p, 1, 2 * p, 0)
            join_plain(T - 1)
            pool.wait_ge(ahead.rec_ready, 1)
            pool.wait_ge(head_done, 2 * ITER - 1)
            for u in range(2):
                nc.gpsimd.tensor_tensor(ahead.ht[:, u].rearrange("p (h d) -> p h d", h=H), hid[:, u, :, 0:DH],
                                        spread(ahead.rec[:, u, :][:, :, None], [P, H, DH]),
                                        ALU.mult).then_inc(ahead.h_ready, 1)


class Ahead:

    def __init__(self, nc, ctx, shared, s1b):
        def sem(name):
            return ctx.enter_context(nc.semaphore(name))

        halves = shared.bitcast(fp16)
        self.wf = s1b.rearrange("p a n -> p (a n)").rearrange("p (k n) -> p k n", k=KC)
        self.wh, self.wl = (halves[:, m * KC * D:(m + 1) * KC * D].rearrange("p (k n) -> p k n", k=KC)
                            for m in range(2))
        rest = halves[:, 2 * KC * D:]
        self.ht = rest[:, 0:4 * D].bitcast(fp32).rearrange("p (u n) -> p u n", u=2)
        self.hp = rest[:, 4 * D:8 * D].rearrange("p (u w n) -> p u w n", u=2, w=2)
        self.rec = ctx.enter_context(nc.sbuf_tensor("rec", [P, T, H], fp32))
        self.w_in = [sem(f"w_out_in{k}") for k in range(KC)]
        self.w_high = sem("w_out_high")
        self.w_split = sem("w_out_split")
        self.rec_ready = sem("rec_ready")
        self.h_ready = sem("h_ready")
        self.h_high = sem("h_high")
        self.h_split = sem("h_split")


def finish(nc, x, b_out, w1, b1, out, adjT, hid, ahead):
    ctx = ExitStack()
    with ctx:
        def sb(name, shape, dt):
            return ctx.enter_context(nc.sbuf_tensor(name, shape, dt))

        def pb(name, shape, dt):
            return ctx.enter_context(nc.psum_tensor(name, shape, dt))

        def sem(name):
            return ctx.enter_context(nc.semaphore(name))

        w1f = sb("w1f", [P, KC, D], fp32)
        wh = [ahead.wh, sb("w1h", [P, KC, D], fp16)]
        wl = [ahead.wl, sb("w1l", [P, KC, D], fp16)]
        bias = sb("bias", [P, 2, D], fp32)
        idb = sb("idb2", [P, P], fp16)
        xr = sb("xr", [P, 2, D], fp32)
        rec, ht, hp = ahead.rec, ahead.ht, ahead.hp
        h_t = sb("h_t", [P, 2, 2, KC, P], fp16)
        y = sb("y", [P, 2, D], fp32)
        ye = sb("ye", [P, 2, D], fp32)
        z = sb("z", [P, 2, D], fp32)
        st = sb("st", [P, 2, 6], fp32)
        mv = sb("mv", [P, 2, 2], fp32)
        ve = sb("ve", [P, 2, 1], fp32)
        rs = sb("rs", [P, 2, 1], fp32)
        consts = sb("consts", [P, 2], fp32)
        x1 = hid[:].rearrange("p t h c -> p t (h c)")[:, :, 0:D]
        xp = sb("xp", [P, 2, 2, D], fp16)
        x_t = sb("x_t", [P, 2, 2, KC, P], fp16)
        sh = sb("sh", [P, T, D], fp16)
        sl = sb("sl", [P, T, D], fp16)
        tile = [sb(f"tile_{u}", [P, T, P], u8) for u in range(2)]
        ph = [pb(f"ph{u}", [P, 2, KC, P], fp16) for u in range(2)]
        px = [pb(f"px{u}", [P, 2, KC, P], fp16) for u in range(2)]
        pm = [pb(f"pm{u}", [P, D], fp32) for u in range(2)]
        ps = [pb(f"ps{u}", [P, D], fp32) for u in range(2)]
        po = [p[:].rearrange("p w k n -> p (w k n)").bitcast(fp32) for p in ph]

        w_in = sem("w_in")
        b_in = [sem(f"b_in{m}") for m in range(2)]
        ones_set = sem("ones_set2")
        ident_ready = sem("ident2")
        w_high = sem("w_high2")
        w_split = sem("w_split2")
        x_in = [sem(f"x_in{u}") for u in range(2)]
        tile_in = [sem(f"tile_in{u}") for u in range(2)]
        rec_ready, h_ready, h_high, h_split = ahead.rec_ready, ahead.h_ready, ahead.h_high, ahead.h_split
        h_turned = sem("h_turned")
        h_out = sem("h_out")
        mixed = sem("mixed")
        y_ready = sem("y_ready")
        y_neg = sem("y_neg")
        y_exp = sem("y_exp")
        y_pos = sem("y_pos")
        y_elu = sem("y_elu")
        z_ready = sem("z_ready")
        stats_ready = sem("stats_ready")
        var_ready = sem("var_ready")
        eps_added = sem("eps_added")
        rstd_ready = sem("rstd_ready")
        x1_ready = sem("x1_ready")
        x_high = sem("x_high")
        x_split = sem("x_split2")
        x_turned = sem("x_turned2")
        x_out = sem("x_out")
        supported = sem("supported")
        s_high = sem("s_high")
        s_split = sem("s_split")
        gathered = sem("gathered")
        xb_ready = sem("xb_ready")
        o_sum = sem("o_sum")
        o_ready = sem("o_ready")
        stored = [sem(f"stored{u}") for u in range(2)]
        dve_passed = sem("dve_passed")
        pe_passed = sem("pe_passed2")

        def exists(t):
            return not isinstance(t, int) or 0 <= t < T

        def later(t):
            return not isinstance(t, int) or t >= 2

        def slots(eng, slot, first, last):
            lo, hi = 6, T - 4
            for k in range(first, lo):
                slot(k, k % 2)
            with eng.Fori(lo // 2, hi // 2) as i:
                for u in range(2):
                    slot(2 * i + u, u)
            for k in range(hi, last + 1):
                slot(k, k % 2)

        def over_tiles(eng, slot):
            for u in range(2):
                slot(u, u, 0, True)
            with eng.Fori(1, T // 2) as i:
                for u in range(2):
                    slot(2 * i + u, u, i, False)

        block = ctx.enter_context(nc.Block())

        @block.sync
        def _(sp):
            sp.dma_start(bias[:, 0, :], b_out[None, :].to_broadcast([P, D])).then_inc(b_in[0], 16)
            sp.dma_start(w1f[:], w1.rearrange("(k p) n -> p k n", p=P)).then_inc(w_in, 16)

            def load(t, u, i, first):
                if not first:
                    sp.wait_ge(z_ready, t - 1)
                sp.dma_start(xr[:, u, :], x[t, :, :]).then_inc(x_in[u], 16)

            load(0, 0, 0, True)
            load(1, 1, 0, True)
            sp.dma_start(bias[:, 1, :], b1[None, :].to_broadcast([P, D])).then_inc(b_in[1], 16)
            with sp.Fori(1, T // 2) as i:
                for u in range(2):
                    load(2 * i + u, u, i, False)

            def edges(t, u, i, first):
                if not first:
                    sp.wait_ge(gathered, t - 1)
                sp.dma_start(tile[u][:], adjT[:, t, :, :]).then_inc(tile_in[u], 16)

            over_tiles(sp, edges)

        @block.gpsimd
        def _(pool):
            nc.gpsimd.memset(idb[:], 1.0).then_inc(ones_set, 1)
            nc.gpsimd.memset(consts[:, 0:1], EPS).then_inc(ones_set, 1)
            nc.gpsimd.memset(consts[:, 1:2], -0.5).then_inc(ones_set, 1)
            pool.wait_ge(ones_set, 3)
            nc.gpsimd.affine_select(out=idb[:], in_=idb[:], compare_op=ALU.is_equal, fill=0.0, base=0,
                                    pattern=[[-1, P]], channel_multiplier=1).then_inc(ident_ready, 1)

            def rstd(n, t, u):
                pool.wait_ge(var_ready, n + t + 1)
                nc.gpsimd.tensor_tensor(ve[:, u], mv[:, u, 1:2], consts[:, 0:1], ALU.add).then_inc(eps_added, 1)
                pool.wait_ge(eps_added, n + t + 1)
                nc.gpsimd.tensor_tensor(rs[:, u], ve[:, u], consts[:, 1:2], ALU.pow).then_inc(rstd_ready, 1)

            def normalise(t, u):
                if isinstance(t, int) and t == TH:
                    pool.wait_ge(rec_ready, 2)
                if later(t):
                    pool.wait_ge(h_split, t - 1)
                nc.gpsimd.tensor_tensor(ht[:, u, :].rearrange("p (h d) -> p h d", h=H), hid[:, t, :, 0:DH],
                                        spread(rec[:, t, :][:, :, None], [P, H, DH]), ALU.mult).then_inc(h_ready, 1)

            def residual(t, u, i):
                pool.wait_ge(x_in[u], 16 * i + 16)
                if later(t):
                    pool.wait_ge(x1_ready, t - 1)
                pool.wait_ge(y_elu, t + 1)
                nc.gpsimd.tensor_tensor(z[:, u], ye[:, u], xr[:, u], ALU.add).then_inc(z_ready, 1)

            def slot(k, u, i):
                if exists(k):
                    residual(k, u, i)
                    rstd(0, k, u)
                if exists(k + 4):
                    normalise(k + 4, u)

            for k in range(-2, TH - 2):
                slot(k, k % 2, k // 2)
            with pool.Fori(TH // 2 - 1, T // 2 - 2) as i:
                for u in range(2):
                    slot(2 * i + u, u, i)
            for k in range(T - 4, T):
                slot(k, k % 2, k // 2)

            def with_bias(t, u, i, first):
                if not first:
                    pool.wait_ge(o_sum, t - 1)
                nc.gpsimd.tensor_tensor(ye[:, u], x1[:, t, :], bias[:, 1, :], ALU.add).then_inc(xb_ready, 1)

            pool.wait_ge(x1_ready, T)
            pool.wait_ge(b_in[1], 16)
            with_bias(0, 0, 0, True)
            with_bias(1, 1, 0, True)
            rstd(T, 0, 0)
            with_bias(2, 0, 1, False)
            rstd(T, 1, 1)
            with pool.Fori(1, T // 2 - 1) as i:
                for u in range(2):
                    with_bias(2 * i + u + 1, 1 - u, i, False)
                    rstd(T, 2 * i + u, u)
            with_bias(T - 1, 1, 0, False)
            rstd(T, T - 2, 0)
            rstd(T, T - 1, 1)

        @block.scalar
        def _(act):
            def h_cast(t, u):
                act.wait_ge(h_ready, t + 1)
                if later(t):
                    act.wait_ge(h_turned, t - 1)
                nc.scalar.activation(hp[:, u, 0], ht[:, u], ACT.Copy).then_inc(h_high, 1)

            def h_evict(t, u):
                act.wait_ge(h_turned, t + 1)
                if later(t):
                    act.wait_ge(mixed, t - 1)
                nc.scalar.activation(h_t[:, u].rearrange("p w k n -> p (w k n)"),
                                     ph[u][:].rearrange("p w k n -> p (w k n)"), ACT.Copy).then_inc(h_out, 1)

            def elu(t, u):
                act.wait_ge(y_ready, t + 1)
                if later(t):
                    act.wait_ge(z_ready, t - 1)
                nc.scalar.activation(ye[:, u], y[:, u], ACT.Relu, scale=-1.0).then_inc(y_neg, 1)
                act.wait_ge(y_neg, t + 1)
                nc.scalar.activation(ye[:, u], ye[:, u], ACT.Exp, scale=-1.0).then_inc(y_exp, 1)

            def x_cast(t, u):
                act.wait_ge(x1_ready, t + 1)
                if later(t):
                    act.wait_ge(x_turned, t - 1)
                nc.scalar.activation(xp[:, u, 0], x1[:, t, :], ACT.Copy).then_inc(x_high, 1)

            def x_evict(t, u):
                act.wait_ge(x_turned, t + 1)
                if later(t):
                    act.wait_ge(supported, t - 1)
                nc.scalar.activation(x_t[:, u].rearrange("p w k n -> p (w k n)"),
                                     px[u][:].rearrange("p w k n -> p (w k n)"), ACT.Copy).then_inc(x_out, 1)

            def s_out(t, u):
                act.wait_ge(supported, t + 1)
                nc.scalar.activation(sh[:, t, :], ps[u][:], ACT.Copy).then_inc(s_high, 1)

            def slot(k, u):
                for stage, t in ((elu, k), (x_cast, k - 1), (h_cast, k + 3), (h_evict, k + 2), (s_out, k - 3),
                                 (x_evict, k - 2)):
                    if exists(t):
                        stage(t, (u + (t - k)) % 2)

            act.wait_ge(ones_set, 3)
            nc.scalar.activation(ve[:, 0], consts[:, 1:2], ACT.Exp)
            h_evict(0, 0)
            h_evict(1, 1)
            h_cast(2, 0)
            act.wait_ge(w_in, 16)
            nc.scalar.activation(wh[1][:], w1f[:], ACT.Copy, scale=UP).then_inc(w_high, 1)
            slots(act, slot, 0, T + 2)

            def store(t, u, i, first):
                act.wait_ge(o_ready, t + 1)
                act.dma_start(out[t, :, :], y[:, u]).then_inc(stored[u], 16)

            over_tiles(act, store)
            for u in range(2):
                act.wait_ge(stored[u], 16 * (T // 2))

        @block.vector
        def _(dve):
            def h_low(t, u):
                dve.wait_ge(h_high, t + 1)
                nc.vector.tensor_tensor(hp[:, u, 1], ht[:, u], hp[:, u, 0], ALU.subtract).then_inc(h_split, 1)

            def biased(t, u):
                dve.wait_ge(mixed, t + 1)
                nc.vector.scalar_tensor_tensor(y[:, u], pm[u][:], 1.0 / UP, bias[:, 0, :], ALU.mult,
                                               ALU.add).then_inc(y_ready, 1)

            def elu(t, u):
                dve.wait_ge(y_exp, t + 1)
                nc.vector.tensor_scalar(y[:, u], y[:, u], 0.0, -1.0, ALU.max, ALU.add).then_inc(y_pos, 1)
                dve.wait_ge(y_pos, t + 1)
                nc.vector.tensor_tensor(ye[:, u], y[:, u], ye[:, u], ALU.add).then_inc(y_elu, 1)

            def stats(n, t, u, ready):
                dve.wait_ge(ready, t + 1)
                nc.vector.bn_stats(st[:, u], z[:, u]).then_inc(stats_ready, 1)
                dve.wait_ge(stats_ready, n + t + 1).then_inc(dve_passed, 1)
                nc.vector.bn_aggr(mv[:, u], st[:, u]).then_inc(var_ready, 1)

            def norm(n, t, u, dst, ready):
                dve.wait_ge(rstd_ready, n + t + 1)
                nc.vector.tensor_scalar(dst, z[:, u], mv[:, u, 0:1], rs[:, u], ALU.subtract,
                                        ALU.mult).then_inc(ready, 1)

            def x_low(t, u):
                dve.wait_ge(x_high, t + 1)
                nc.vector.tensor_tensor(xp[:, u, 1], x1[:, t, :], xp[:, u, 0], ALU.subtract).then_inc(x_split, 1)

            def s_low(t, u):
                dve.wait_ge(s_high, t + 1)
                nc.vector.tensor_tensor(sl[:, t, :], ps[u][:], sh[:, t, :], ALU.subtract).then_inc(s_split, 1)

            def slot(k, u):
                if exists(k):
                    biased(k, u)
                if exists(k - 1):
                    norm(0, k - 1, 1 - u, x1[:, k - 1, :], x1_ready)
                if isinstance(k, int) and k == 0:
                    dve.wait_ge(w_high, 1)
                    nc.vector.scalar_tensor_tensor(wl[1][:], w1f[:], UP, wh[1][:], ALU.mult,
                                                   ALU.subtract).then_inc(w_split, 1)
                if exists(k):
                    elu(k, u)
                if exists(k - 1):
                    x_low(k - 1, 1 - u)
                if exists(k + 3):
                    h_low(k + 3, 1 - u)
                if exists(k):
                    stats(0, k, u, z_ready)
                if exists(k - 3):
                    s_low(k - 3, 1 - u)

            nc.vector.reciprocal(rec[:, TH:T], hid[:, TH:T, :, DH]).then_inc(rec_ready, 1)
            h_low(2, 0)
            dve.wait_ge(b_in[0], 16)
            slots(dve, slot, 0, T + 2)

            def second(t, u):
                dve.wait_ge(gathered, t + 1)
                dve.wait_ge(xb_ready, t + 1)
                nc.vector.scalar_tensor_tensor(z[:, u], po[u], 1.0 / UP, ye[:, u], ALU.mult,
                                               ALU.add).then_inc(o_sum, 1)

            def normed(t, u, i, first):
                second(t, u)
                stats(T, t, u, o_sum)
                if not first:
                    dve.wait_ge(stored[u], 16 * i)
                norm(T, t, u, y[:, u], o_ready)

            over_tiles(dve, normed)

        @block.tensor
        def _(pe):
            def product(to, parts, w, k):
                for q, (lhs, rhs) in enumerate(((0, wh[w]), (0, wl[w]), (1, wh[w]))):
                    last = nc.tensor.matmul(to[:], parts[:, lhs, k, :], rhs[:, k, :],
                                            start=(k == 0 and q == 0), stop=(k == KC - 1 and q == 2))
                return last

            def turn(rows, to):
                for w in range(2):
                    for k in range(KC):
                        last = nc.tensor.transpose(to[:, w, k, :], rows[:, w, k * P:(k + 1) * P], idb[:])
                return last

            def h_turn(t, u):
                pe.wait_ge(h_split, t + 1)
                if later(t):
                    pe.wait_ge(h_out, t - 1)
                turn(hp[:, u], ph[u]).then_inc(h_turned, 1)

            def mix(t, u):
                pe.wait_ge(h_out, t + 1)
                if later(t):
                    pe.wait_ge(y_ready, t - 1)
                for k in range(KC):
                    last = product(pm[u], h_t[:, u], 0, k)
                last.then_inc(mixed, 1)

            def x_turn(t, u):
                pe.wait_ge(x_split, t + 1)
                if later(t):
                    pe.wait_ge(x_out, t - 1)
                turn(xp[:, u], px[u]).then_inc(x_turned, 1)

            def support(t, u):
                pe.wait_ge(x_out, t + 1)
                if later(t):
                    pe.wait_ge(s_split, t - 1)
                if isinstance(t, int) and t == 0:
                    pe.wait_ge(w_split, 1)
                for k in range(KC):
                    last = product(ps[u], x_t[:, u], 1, k)
                last.then_inc(supported, 1)

            def gather(u, js):
                for j in js:
                    for q, s in enumerate((sh, sl)):
                        last = nc.tensor.matmul(po[u], tile[u][:, j, :].bitcast(fp8), s[:, j, :],
                                                start=(j == 0 and q == 0), stop=(j == T - 1 and q == 1))
                return last

            def slot(k, u):
                for stage, t in ((mix, k), (h_turn, k + 2), (support, k - 3), (x_turn, k - 2)):
                    if exists(t):
                        stage(t, (u + (t - k)) % 2)

            pe.wait_ge(ident_ready, 1)
            h_turn(0, 0)
            h_turn(1, 1)
            slots(pe, slot, 0, T - 1)
            pe.wait_ge(tile_in[0], 16)
            pe.wait_ge(h_out, T)
            pe.wait_ge(s_split, T - 5)
            gather(0, range(0, T // 4))
            support(T - 3, 1)
            gather(0, range(T // 4, T // 2))
            x_turn(T - 2, 0)
            support(T - 2, 0)
            x_turn(T - 1, 1)
            pe.wait_ge(s_split, T - 4)
            gather(0, range(T // 2, T - 4))
            support(T - 1, 1)
            pe.wait_ge(s_split, T - 1)
            gather(0, range(T - 4, T - 1))
            pe.wait_ge(s_split, T)
            gather(0, range(T - 1, T)).then_inc(gathered, 1)
            pe.wait_ge(tile_in[1], 16)
            gather(1, range(T)).then_inc(gathered, 1)
            with pe.Fori(1, T // 2) as i:
                for u in range(2):
                    t = 2 * i + u
                    pe.wait_ge(tile_in[u], 16 * i + 16).then_inc(pe_passed, 1)
                    pe.wait_ge(o_sum, t - 1).then_inc(pe_passed, 1)
                    gather(u, range(T)).then_inc(gathered, 1)


def gat_gcn(nc, x, adj, w_seq, a1, a2, w_out, b_out, w1, b1, out):
    s1_rows = nc.dram_tensor("s1_rows", [H, N], fp32, kind="Internal").ap()
    x_t = x.rearrange("(t p) d -> t p d", p=P)
    adj_t = adj.rearrange("(t p) n -> t p n", p=P)
    out_t = out.rearrange("(t p) d -> t p d", p=P)
    with ExitStack() as ctx:
        adjT = ctx.enter_context(nc.sbuf_tensor("adjT", [P, T, T, P], u8))
        hid = ctx.enter_context(nc.sbuf_tensor("hid", [P, T, H, C], fp32))
        s1b = ctx.enter_context(nc.sbuf_tensor("s1b", [P, 2, NH], fp32))
        shared = ctx.enter_context(nc.sbuf_tensor("shared", [P, T * NH], u8))
        ahead = Ahead(nc, ctx, shared[:], s1b[:])
        with ExitStack() as mid:
            AB = mid.enter_context(nc.sbuf_tensor("AB", [P, T, 2, H], fp32))
            S2 = mid.enter_context(nc.sbuf_tensor("S2", [P, H, 2, T], fp32))
            V = mid.enter_context(nc.sbuf_tensor("V", [P, H, T, CW], fp16))
            s2c = [mid.enter_context(nc.sbuf_tensor(f"s2c{a}", [P, 2, T], fp32)) for a in range(2)]
            heads = [s1b[:, a] for a in range(2)]
            project_nodes(nc, x_t, adj_t, w_seq, a1, a2, s1_rows, adjT, hid, V, AB, S2, heads, s2c, shared[:])
            attend(nc, s1_rows, w_out, adjT, V, AB, S2, heads, s2c, shared[:], hid, ahead)
        finish(nc, x_t, b_out, w1, b1, out_t, adjT, hid, ahead)


_INS = ['x', 'adj', 'L0_gnn_W_seq', 'L0_gnn_a1', 'L0_gnn_a2', 'L0_gnn_W_out', 'L0_gnn_b_out',
        'L1_gnn_weight', 'L1_gnn_bias']
_OUTS = [((2048, 512), 'float32')]


def kernel(**inputs):
    import numpy as _np
    import concourse.bacc as _bacc
    from concourse import mybir as _mybir
    from concourse.bass_utils import run_bass_kernel_spmd as _run

    nc = _bacc.Bacc("TRN2", target_bir_lowering=False, num_devices=1)
    arrays, args = {}, []
    for name in _INS:
        a = _np.ascontiguousarray(inputs[name])
        arrays[f"in_{name}_dram"] = a
        args.append(nc.dram_tensor(f"in_{name}_dram", a.shape, _mybir.dt.from_np(a.dtype), kind="ExternalInput").ap())
    for i, (shape, dtype) in enumerate(_OUTS):
        dt = _mybir.dt.from_np(_np.dtype(dtype))
        args.append(nc.dram_tensor(f"out_{i}_dram", shape, dt, kind="ExternalOutput").ap())
    gat_gcn(nc, *args)
    r = _run(nc, [arrays], core_ids=[0])
    return r.results[0]["out_0_dram"]
```
